# Optimizing a Trainium2 kernel written in Bass

```python
import numpy as np
import jax
import jax.numpy as jnp

def _softmax(x, axis=-1):
    return jax.nn.softmax(x, axis=axis)

def _gelu(x):
    return jax.nn.gelu(x, approximate=True)

def _silu(x):
    return jax.nn.silu(x)

def _sigmoid(x):
    return jax.nn.sigmoid(x)

def _layernorm(x, axis=-1, eps=1e-05):
    m = jnp.mean(x, axis=axis, keepdims=True)
    v = jnp.var(x, axis=axis, keepdims=True)
    return (x - m) / jnp.sqrt(v + eps)

def _scatter_add(tgt, idx, src, axis=0):
    return tgt.at[idx].add(src)

def _segment_sum(src, seg, n):
    return jax.ops.segment_sum(src, seg, n)
kernel_name = 'mk_pixart_resid_d2_seqx_r2_9dcc82'

def setup_inputs(seed: int=0):
    np.random.seed(seed)
    _w = jnp.asarray

    def _rec_inputs():
        import jax
        import jax.numpy as jnp
        _rk = jax.random.key(seed)
        x = -0.0002928 + 1 * jax.random.normal(jax.random.fold_in(_rk, 1), (4, 2048, 512), jnp.float32)
        _lenS = 2048 - jax.random.randint(jax.random.fold_in(_rk, 7), (4,), 0, max(1, 2048 // 4) + 1, jnp.int32)
        _lenS2 = 154 - jax.random.randint(jax.random.fold_in(_rk, 8), (4,), 0, max(1, 154 // 4) + 1, jnp.int32)
        _ctx_1024P = jax.random.normal(jax.random.fold_in(_rk, 11), (4, 16, 512), jnp.float32)
        _ctx_1024c = jax.random.dirichlet(jax.random.fold_in(_rk, 511), 0.3 * jnp.ones((16,), jnp.float32), (4, 154))
        _ctx_1024t = jnp.einsum('bsk,bkd->bsd', _ctx_1024c, _ctx_1024P)
        _ctx_1024t = _ctx_1024t * jax.lax.rsqrt(jnp.mean(jnp.square(_ctx_1024t)) + 1e-12) * 0.953939
        ctx_1024 = -1.39393e-06 + 0.999914 * (_ctx_1024t + 0.3 * jax.random.normal(jax.random.fold_in(_rk, 611), (4, 154, 512), jnp.float32))
        condB_tau = jax.random.uniform(jax.random.fold_in(_rk, 12), (4,), jnp.float32, 0.0, 1.23395)
        fside_BxS2_0 = -0.00205293 + 0.99739 * jax.random.normal(jax.random.fold_in(_rk, 13), (4, 154), jnp.float32)
        return (x, ctx_1024, condB_tau, fside_BxS2_0)
    x, ctx_1024, condB_tau, fside_BxS2_0 = _rec_inputs()

    def _L0_xcond_setup():
        import jax, jax.numpy as jnp
        import numpy as np
        B, S, D, H = (2, 1024, 512, 16)
        DK = D // H

        def _split_heads(x):
            b, s, _ = x.shape
            return x.reshape(b, s, H, DK).transpose(0, 2, 1, 3)
        key = jax.random.key(seed)
        ks = jax.random.split(key, 14)
        inp = {'query': jax.random.normal(ks[0], (B, S, D), jnp.float32), 'key': jax.random.normal(ks[1], (B, S, D), jnp.float32), 'value': jax.random.normal(ks[2], (B, S, D), jnp.float32), 'tau': jax.random.uniform(ks[3], (B, 1), jnp.float32, 0.5, 1.5), 'delta': jax.random.normal(ks[4], (B, S), jnp.float32)}
        sc = 1.0 / np.sqrt(D)
        for i, name in enumerate(['q', 'k', 'v', 'o']):
            inp[f'W{name}'] = jax.random.normal(ks[5 + 2 * i], (D, D), jnp.float32) * sc
            inp[f'b{name}'] = jax.random.normal(ks[6 + 2 * i], (D,), jnp.float32) * 0.01
        return inp
    _L0_xcond_all = _L0_xcond_setup()
    _L0_xcond_in = {k: v for k, v in _L0_xcond_all.items() if k in ('Wq', 'bq', 'Wk', 'bk', 'Wv', 'bv', 'Wo', 'bo')}
    del _L0_xcond_all

    def _L0_ffn_setup():
        import jax, jax.numpy as jnp
        import numpy as np
        TOP_K = 8
        NUM_EXPERTS = 32
        CAPACITY = 512
        key = jax.random.key(seed)
        k1, k2, k3, k4 = jax.random.split(key, 4)
        B, S, H, E, F = (2, 512, 512, NUM_EXPERTS, 384)
        return {'hidden_states': jax.random.normal(k1, (B, S, H), dtype=jnp.float32), 'gate_weight': jax.random.normal(k2, (E, H), dtype=jnp.float32) * 0.02, 'gate_up_proj': jax.random.normal(k3, (E, 2 * F, H), dtype=jnp.float32) * 0.02, 'down_proj': jax.random.normal(k4, (E, H, F), dtype=jnp.float32) * 0.02}
    _L0_ffn_all = _L0_ffn_setup()
    _L0_ffn_in = {k: v for k, v in _L0_ffn_all.items() if k in ('gate_weight', 'gate_up_proj', 'down_proj')}
    del _L0_ffn_all

    def _L1_xcond_setup():
        import jax, jax.numpy as jnp
        import numpy as np
        D_MODEL = 512
        N_HEADS = 16
        key = jax.random.key(seed)
        ks = jax.random.split(key, 16)
        B, L, S, D = (4, 1024, 1024, D_MODEL)
        inp = {'q': jax.random.normal(ks[0], (B, L, D), jnp.float32), 'k': jax.random.normal(ks[1], (B, S, D), jnp.float32), 'v': jax.random.normal(ks[2], (B, S, D), jnp.float32), 'tau': jax.random.uniform(ks[3], (B, 1), jnp.float32, 0.5, 1.5), 'delta': jax.random.normal(ks[4], (B, S), jnp.float32)}
        s = 1.0 / np.sqrt(D)
        inp['Wq'] = jax.random.normal(ks[5], (D, D), jnp.float32) * s
        inp['bq'] = jnp.zeros((D,), jnp.float32)
        inp['Wk'] = jax.random.normal(ks[6], (D, D), jnp.float32) * s
        inp['bk'] = jnp.zeros((D,), jnp.float32)
        inp['Wv'] = jax.random.normal(ks[7], (D, D), jnp.float32) * s
        inp['bv'] = jnp.zeros((D,), jnp.float32)
        inp['Wo'] = jax.random.normal(ks[8], (D, D), jnp.float32) * s
        inp['bo'] = jnp.zeros((D,), jnp.float32)
        return inp
    _L1_xcond_all = _L1_xcond_setup()
    _L1_xcond_in = {k: v for k, v in _L1_xcond_all.items() if k in ('Wq', 'bq', 'Wk', 'bk', 'Wv', 'bv', 'Wo', 'bo')}
    del _L1_xcond_all

    def _L1_ffn_setup():
        import jax, jax.numpy as jnp
        import numpy as np
        DIM = 512
        NUM_HEAVY = 512
        N_ITERS = 50
        EPS = 1.0
        FETCH_K_RATIO = 9.0 / 8.0

        def rms_norm(x, gamma):
            norm = jnp.maximum(jnp.linalg.norm(x, axis=-1, keepdims=True), 1e-12)
            return x / norm * x.shape[-1] ** 0.5 * gamma

        def feed_forward(x, gamma, w1, b1, w2, b2):
            h = jax.nn.gelu(rms_norm(x, gamma) @ w1 + b1, approximate=False)
            return h @ w2 + b2

        def coor_descent(s, k, n_iters, eps):
            logk = jnp.log(jnp.asarray(k, dtype=s.dtype))

            def step(ab, _):
                a, b = ab
                sb = (s + b) / eps
                a = eps * (logk - jax.scipy.special.logsumexp(sb, axis=-1, keepdims=True))
                b = -jax.nn.relu(s + a)
                return ((a, b), None)
            a0 = jnp.zeros_like(s[..., :1])
            b0 = -s
            (a, b), _ = jax.lax.scan(step, (a0, b0), None, length=n_iters)
            return jnp.exp((s + a + b) / eps)
        key = jax.random.key(seed)
        ks = jax.random.split(key, 8)
        b, n, d = (4, 4096, DIM)
        dl, dh = (int(d * 0.5), d * 4)
        u = lambda k, shape, fan_in: jax.random.uniform(k, shape, jnp.float32, -1.0, 1.0) / np.sqrt(fan_in)
        return {'x': jax.random.normal(ks[0], (b, n, d), jnp.float32), 'routing_token': jax.random.normal(ks[1], (d,), jnp.float32), 'light_gamma': jnp.ones((d,), jnp.float32), 'light_w1': u(ks[2], (d, dl), d), 'light_b1': jnp.zeros((dl,), jnp.float32), 'light_w2': u(ks[3], (dl, d), dl), 'light_b2': jnp.zeros((d,), jnp.float32), 'heavy_gamma': jnp.ones((d,), jnp.float32), 'heavy_w1': u(ks[4], (d, dh), d), 'heavy_b1': jnp.zeros((dh,), jnp.float32), 'heavy_w2': u(ks[5], (dh, d), dh), 'heavy_b2': jnp.zeros((d,), jnp.float32)}
    _L1_ffn_all = _L1_ffn_setup()
    _L1_ffn_in = {k: v for k, v in _L1_ffn_all.items() if k in ('routing_token', 'light_gamma', 'light_w1', 'light_b1', 'light_w2', 'light_b2', 'heavy_gamma', 'heavy_w1', 'heavy_b1', 'heavy_w2', 'heavy_b2')}
    del _L1_ffn_all
    return {'x': x, 'ctx_1024': ctx_1024, 'condB_tau': condB_tau, 'fside_BxS2_0': fside_BxS2_0, 'L0_xcond_Wq': _L0_xcond_in['Wq'], 'L0_xcond_bq': _L0_xcond_in['bq'], 'L0_xcond_Wk': _L0_xcond_in['Wk'], 'L0_xcond_bk': _L0_xcond_in['bk'], 'L0_xcond_Wv': _L0_xcond_in['Wv'], 'L0_xcond_bv': _L0_xcond_in['bv'], 'L0_xcond_Wo': _L0_xcond_in['Wo'], 'L0_xcond_bo': _L0_xcond_in['bo'], 'L0_ffn_gate_weight': _L0_ffn_in['gate_weight'], 'L0_ffn_gate_up_proj': _L0_ffn_in['gate_up_proj'], 'L0_ffn_down_proj': _L0_ffn_in['down_proj'], 'L1_xcond_Wq': _L1_xcond_in['Wq'], 'L1_xcond_bq': _L1_xcond_in['bq'], 'L1_xcond_Wk': _L1_xcond_in['Wk'], 'L1_xcond_bk': _L1_xcond_in['bk'], 'L1_xcond_Wv': _L1_xcond_in['Wv'], 'L1_xcond_bv': _L1_xcond_in['bv'], 'L1_xcond_Wo': _L1_xcond_in['Wo'], 'L1_xcond_bo': _L1_xcond_in['bo'], 'L1_ffn_routing_token': _L1_ffn_in['routing_token'], 'L1_ffn_light_gamma': _L1_ffn_in['light_gamma'], 'L1_ffn_light_w1': _L1_ffn_in['light_w1'], 'L1_ffn_light_b1': _L1_ffn_in['light_b1'], 'L1_ffn_light_w2': _L1_ffn_in['light_w2'], 'L1_ffn_light_b2': _L1_ffn_in['light_b2'], 'L1_ffn_heavy_gamma': _L1_ffn_in['heavy_gamma'], 'L1_ffn_heavy_w1': _L1_ffn_in['heavy_w1'], 'L1_ffn_heavy_b1': _L1_ffn_in['heavy_b1'], 'L1_ffn_heavy_w2': _L1_ffn_in['heavy_w2'], 'L1_ffn_heavy_b2': _L1_ffn_in['heavy_b2']}

def reference(x, ctx_1024, condB_tau, fside_BxS2_0, L0_xcond_Wq, L0_xcond_bq, L0_xcond_Wk, L0_xcond_bk, L0_xcond_Wv, L0_xcond_bv, L0_xcond_Wo, L0_xcond_bo, L0_ffn_gate_weight, L0_ffn_gate_up_proj, L0_ffn_down_proj, L1_xcond_Wq, L1_xcond_bq, L1_xcond_Wk, L1_xcond_bk, L1_xcond_Wv, L1_xcond_bv, L1_xcond_Wo, L1_xcond_bo, L1_ffn_routing_token, L1_ffn_light_gamma, L1_ffn_light_w1, L1_ffn_light_b1, L1_ffn_light_w2, L1_ffn_light_b2, L1_ffn_heavy_gamma, L1_ffn_heavy_w1, L1_ffn_heavy_b1, L1_ffn_heavy_w2, L1_ffn_heavy_b2):
    import jax
    import jax.numpy as jnp

    def _L0_xcond_ref(query, key, value, tau, delta, Wq, bq, Wk, bk, Wv, bv, Wo, bo):
        import jax, jax.numpy as jnp
        import numpy as np
        B, S, D, H = (2, 1024, 512, 16)
        DK = D // H

        def _split_heads(x):
            b, s, _ = x.shape
            return x.reshape(b, s, H, DK).transpose(0, 2, 1, 3)
        q = _split_heads(query @ Wq.T + bq)
        k = _split_heads(key @ Wk.T + bk)
        v = _split_heads(value @ Wv.T + bv)
        scores = jnp.einsum('bhqd,bhkd->bhqk', q, k)
        scores = scores * tau[:, :, None, None] + delta[:, None, None, :]
        scores = scores / jnp.sqrt(jnp.asarray(DK, scores.dtype))
        p_attn = jax.nn.softmax(scores, axis=-1)
        x = jnp.einsum('bhqk,bhkd->bhqd', p_attn, v)
        x = x.transpose(0, 2, 1, 3).reshape(query.shape[0], -1, H * DK)
        return x @ Wo.T + bo

    def _L0_ffn_ref(hidden_states, gate_weight, gate_up_proj, down_proj):
        import jax, jax.numpy as jnp
        import numpy as np
        TOP_K = 8
        NUM_EXPERTS = 32
        CAPACITY = 512
        B, S, H = hidden_states.shape
        E = gate_weight.shape[0]
        N = B * S
        x = hidden_states.reshape(N, H)
        logits = x @ gate_weight.T
        probs = jax.nn.softmax(logits.astype(jnp.float32), axis=-1)
        topw, topi = jax.lax.top_k(probs, TOP_K)
        topw = topw / topw.sum(-1, keepdims=True)
        topw = topw.astype(x.dtype)
        flat_e = topi.reshape(-1)
        flat_w = topw.reshape(-1)
        flat_x = jnp.repeat(x, TOP_K, axis=0)
        oh = jax.nn.one_hot(flat_e, E, dtype=jnp.int32)
        pos = (jnp.cumsum(oh, axis=0) * oh).sum(-1) - 1
        buf = jnp.zeros((E, CAPACITY, H), x.dtype).at[flat_e, pos].set(flat_x, mode='drop')
        gu = jnp.einsum('ech,efh->ecf', buf, gate_up_proj)
        gate, up = jnp.split(gu, 2, axis=-1)
        h = jax.nn.silu(gate) * up
        eo = jnp.einsum('ecf,ehf->ech', h, down_proj)
        tok_out = eo.at[flat_e, pos].get(mode='fill', fill_value=0)
        out = (tok_out * flat_w[:, None]).reshape(N, TOP_K, H).sum(1)
        return out.reshape(B, S, H)

    def _L1_xcond_ref(q, k, v, tau, delta, Wq, bq, Wk, bk, Wv, bv, Wo, bo):
        import jax, jax.numpy as jnp
        import numpy as np
        D_MODEL = 512
        N_HEADS = 16
        B, L, D = q.shape
        S = k.shape[1]
        H = N_HEADS
        E = D // H
        qh = (q @ Wq.T + bq).reshape(B, L, H, E)
        kh = (k @ Wk.T + bk).reshape(B, S, H, E)
        vh = (v @ Wv.T + bv).reshape(B, S, H, E)
        scale = 1.0 / np.sqrt(E).astype(np.float32)
        scores = jnp.einsum('blhe,bshe->bhls', qh, kh)
        scores = scores * tau[:, None, None, :] + delta[:, None, None, :]
        a = jax.nn.softmax(scale * scores, axis=-1)
        out = jnp.einsum('bhls,bshd->blhd', a, vh).reshape(B, L, D)
        return out @ Wo.T + bo

    def _L1_ffn_ref(x, routing_token, light_gamma, light_w1, light_b1, light_w2, light_b2, heavy_gamma, heavy_w1, heavy_b1, heavy_w2, heavy_b2):
        import jax, jax.numpy as jnp
        import numpy as np
        DIM = 512
        NUM_HEAVY = 512
        N_ITERS = 50
        EPS = 1.0
        FETCH_K_RATIO = 9.0 / 8.0

        def rms_norm(x, gamma):
            norm = jnp.maximum(jnp.linalg.norm(x, axis=-1, keepdims=True), 1e-12)
            return x / norm * x.shape[-1] ** 0.5 * gamma

        def feed_forward(x, gamma, w1, b1, w2, b2):
            h = jax.nn.gelu(rms_norm(x, gamma) @ w1 + b1, approximate=False)
            return h @ w2 + b2

        def coor_descent(s, k, n_iters, eps):
            logk = jnp.log(jnp.asarray(k, dtype=s.dtype))

            def step(ab, _):
                a, b = ab
                sb = (s + b) / eps
                a = eps * (logk - jax.scipy.special.logsumexp(sb, axis=-1, keepdims=True))
                b = -jax.nn.relu(s + a)
                return ((a, b), None)
            a0 = jnp.zeros_like(s[..., :1])
            b0 = -s
            (a, b), _ = jax.lax.scan(step, (a0, b0), None, length=n_iters)
            return jnp.exp((s + a + b) / eps)
        b, n, d = x.shape
        light_out = feed_forward(x, light_gamma, light_w1, light_b1, light_w2, light_b2)
        s = jnp.einsum('bnd,d->bn', x, routing_token)
        effective_k = min(NUM_HEAVY * FETCH_K_RATIO, n)
        scores = coor_descent(s, effective_k, N_ITERS, EPS)
        sel_scores, sel_idx = jax.lax.top_k(scores, NUM_HEAVY)
        sel_scores = sel_scores + jax.lax.stop_gradient(1.0 - sel_scores)
        routed = jnp.take_along_axis(x, sel_idx[..., None], axis=1)
        routed_out = feed_forward(routed, heavy_gamma, heavy_w1, heavy_b1, heavy_w2, heavy_b2)
        routed_out = routed_out * sel_scores[..., None]
        batch_idx = jnp.arange(b)[:, None]
        heavy_out = jnp.zeros_like(x).at[batch_idx, sel_idx].set(routed_out)
        return light_out + heavy_out
    x = x + _L0_xcond_ref(_layernorm(x, axis=-1), ctx_1024, ctx_1024, condB_tau[:, None], fside_BxS2_0, L0_xcond_Wq, L0_xcond_bq, L0_xcond_Wk, L0_xcond_bk, L0_xcond_Wv, L0_xcond_bv, L0_xcond_Wo, L0_xcond_bo)
    x = x + _L0_ffn_ref(_layernorm(x, axis=-1), L0_ffn_gate_weight, L0_ffn_gate_up_proj, L0_ffn_down_proj)
    x = x + _L1_xcond_ref(_layernorm(x, axis=-1), ctx_1024, ctx_1024, condB_tau[:, None], fside_BxS2_0, L1_xcond_Wq, L1_xcond_bq, L1_xcond_Wk, L1_xcond_bk, L1_xcond_Wv, L1_xcond_bv, L1_xcond_Wo, L1_xcond_bo)
    x = x + _L1_ffn_ref(_layernorm(x, axis=-1), L1_ffn_routing_token, L1_ffn_light_gamma, L1_ffn_light_w1, L1_ffn_light_b1, L1_ffn_light_w2, L1_ffn_light_b2, L1_ffn_heavy_gamma, L1_ffn_heavy_w1, L1_ffn_heavy_b1, L1_ffn_heavy_w2, L1_ffn_heavy_b2)
    return x

_drawn_inputs = setup_inputs


def setup_inputs(seed=0):
    import zlib

    import numpy as np

    out = dict(_drawn_inputs(seed))
    spreads = {'L1_xcond_bq': (0.0, 2.0),
     'L1_xcond_bk': (0.0, 2.0),
     'L1_xcond_bv': (0.0, 0.371),
     'L1_xcond_bo': (0.0, 0.39),
     'L1_ffn_light_gamma': (1.0, 0.6),
     'L1_ffn_light_b1': (0.0, 1.112),
     'L1_ffn_light_b2': (0.0, 0.41),
     'L1_ffn_heavy_gamma': (1.0, 0.6),
     'L1_ffn_heavy_b1': (0.0, 2.0),
     'L1_ffn_heavy_b2': (0.0, 0.774)}
    factors = {'L0_xcond_bq': 8.0,
     'L0_xcond_bk': 64.0,
     'L0_xcond_bv': 6.263,
     'L0_xcond_bo': 6.126,
     'L0_ffn_gate_weight': 6.913,
     'L0_ffn_gate_up_proj': 6.771,
     'L0_ffn_down_proj': 6.478}
    for name, (base, spread) in spreads.items():
        noise = np.random.default_rng([zlib.crc32(name.encode()), seed]).standard_normal(out[name].shape)
        drawn = base * np.exp(spread * noise) if base else spread * noise
        out[name] = jnp.asarray(drawn.astype(out[name].dtype))
    for name, factor in factors.items():
        out[name] = (out[name] * factor).astype(out[name].dtype)
    return out
```

```python
from contextlib import ExitStack
import math

import concourse.bass as bass
from concourse import mybir

F32 = mybir.dt.float32
BF16 = mybir.dt.bfloat16
I32 = mybir.dt.int32
ALU = mybir.AluOpType
ACT = mybir.ActivationFunctionType
AX = mybir.AxisListType.X

P = 128
B, SEQ, D = 4, 2048, 512
NTOK = B * SEQ
KEYS = 154
KTAIL = KEYS - P
HEADS, DK = 16, 32
HG = P // DK
GROUPS = HEADS // HG
TROWS = HG * KTAIL
DC = D // P
TG = 4
GTOK = TG * P
NG = NTOK // GTOK
NT = NTOK // P
E, F, CAP, TOPK = 32, 384, 512, 8
FC = F // P
CC = CAP // P
ROUTED = 512
ITERS = 50
EFF_K = min(ROUTED * 9.0 / 8.0, SEQ)
LIGHT, HEAVY = 256, 2048
HC = HEAVY // P
XW = D + E
XS = D + 4
EPS = 1e-5
UNITS = TG * GROUPS


class Sems:

    def __init__(self, nc, ctx, tag, names):
        self.by = {n: nc.alloc_semaphore(f"{tag}_{n}") for n in names.split()}

        def give_back():
            nc.clear_and_free_semaphores(list(self.by.values()))
            nc.all_engine_barrier()

        ctx.callback(give_back)

    def __getitem__(self, name):
        return self.by[name]


def rows(dram, group, width=None):
    v = dram[bass.ds(group * GTOK, GTOK), 0:width] if width else dram[bass.ds(group * GTOK, GTOK), :]
    return v.rearrange("(s p) d -> p s d", p=P)


def constants(nc, ctx, c):
    c["ident"] = ctx.enter_context(nc.sbuf_tensor("ident", [P, P], F32))
    c["ps"] = ctx.enter_context(nc.psum_tensor("ps", [P, 8, 512], F32))
    with ExitStack() as own:
        s = Sems(nc, own, "cst", "zero")
        block = own.enter_context(nc.Block())

        @block.gpsimd
        def _(pool):
            pool.memset(c["ident"][:], 0.0).then_inc(s["zero"], 1)
            pool.wait_ge(s["zero"], 1)
            pool.affine_select(out=c["ident"][:], in_=c["ident"][:], compare_op=ALU.not_equal, fill=1.0,
                               base=0, pattern=[[-1, P]], channel_multiplier=1)


def key_value_phase(nc, a, scr, c):
    with ExitStack() as ctx:
        def sb(name, shape, dt=F32):
            return ctx.enter_context(nc.sbuf_tensor(f"kv_{name}", shape, dt))

        ctxT = sb("ctxT", [P, DC, B, KEYS])
        wk, wv = sb("wk", [P, DC, D]), sb("wv", [P, DC, D])
        bk, bv = sb("bk", [P, DC]), sb("bv", [P, D])
        tau = sb("tau", [P, B])
        delta = sb("delta", [P, B, KEYS])
        kbd = sb("kbd", [P, B, GROUPS, HG * KEYS])
        vm, vt = sb("vm", [P, B, D]), sb("vt", [KTAIL, B, D])
        zero = sb("zero", [TROWS, D])
        ps = c["ps"]
        s = Sems(nc, ctx, "kv", "zeroed ctx_in w_in scaled matmul evacuated cleared stored")
        JOBS = 16
        block = ctx.enter_context(nc.Block())

        @block.sync
        def _(sp):
            for b in range(B):
                sp.dma_start(ctxT[:, :, b, :],
                             a["ctxT"][b].rearrange("(k p) n -> p k n", p=P)).then_inc(s["ctx_in"], 16)
            sp.dma_start(tau[:], a["tau"].partition_broadcast(P)).then_inc(s["ctx_in"], 16)
            sp.dma_start(delta[:], a["delta"].rearrange("b n -> (b n)").partition_broadcast(P)
                         .rearrange("p (b n) -> p b n", b=B)).then_inc(s["ctx_in"], 16)
            sp.wait_ge(s["zeroed"], 2)
            for l in range(2):
                for b in range(B):
                    sp.dma_start(scr[f"vt{l}"][b], zero[:]).then_inc(s["cleared"], 16)
            sp.wait_ge(s["cleared"], 16 * 2 * B)
            for l in range(2):
                sp.wait_ge(s["evacuated"], JOBS * l)
                sp.dma_start(wk[:], a[f"WkT{l}"].rearrange("(k p) n -> p k n", p=P)).then_inc(s["w_in"], 16)
                sp.dma_start(wv[:], a[f"WvT{l}"].rearrange("(k p) n -> p k n", p=P)).then_inc(s["w_in"], 16)
                sp.dma_start(bv[:], a[f"bv{l}"].partition_broadcast(P)).then_inc(s["w_in"], 16)
                with nc.allow_non_contiguous_dma(reason="a bias by partition"):
                    sp.dma_start(bk[:], a[f"bk{l}"].rearrange("(k p) -> p k", p=P)).then_inc(s["w_in"], 16)
                sp.wait_ge(s["evacuated"], JOBS * (l + 1))
                for b in range(B):
                    sp.dma_start(scr[f"kbd{l}"][b], kbd[:, b]).then_inc(s["stored"], 16)
                    sp.dma_start(scr[f"vm{l}"][b], vm[:, b]).then_inc(s["stored"], 16)
                    for h in range(HG):
                        sp.dma_start(
                            scr[f"vt{l}"][b].rearrange("(n h) (g e d) -> n h g e d", h=HG, e=HG, d=DK)[:, h, :, h, :],
                            vt[:, b].rearrange("n (g e d) -> n g e d", e=HG, d=DK)[:, :, h, :],
                        ).then_inc(s["stored"], 16)
            sp.wait_ge(s["scaled"], 2)
            for b in range(B):
                sp.dma_start(scr["delta"][b], delta[:, b]).then_inc(s["stored"], 16)
            sp.wait_ge(s["stored"], 16 * (2 * (2 + HG) * B + B))

        @block.tensor
        def _(pe):
            pe.wait_ge(s["ctx_in"], 16 * (B + 2))
            for l in range(2):
                pe.wait_ge(s["w_in"], 64 * (l + 1))
                for j in range(JOBS):
                    bank = j % 8
                    if JOBS * l + j >= 8:
                        pe.wait_ge(s["evacuated"], JOBS * l + j - 7)
                    if j < 8:
                        n, half = j // 2, j % 2
                        for k in range(DC):
                            mm = pe.matmul(ps[:, bank, 0:2 * KEYS], wk[:, k, n * P:(n + 1) * P],
                                           ctxT[:, k, 2 * half:2 * half + 2, 0:KEYS],
                                           start=(k == 0), stop=(k == DC - 1))
                    elif j < 12:
                        for k in range(DC):
                            mm = pe.matmul(ps[:, bank, :], ctxT[:, k, j - 8, 0:P], wv[:, k, :],
                                           start=(k == 0), stop=(k == DC - 1))
                    else:
                        for k in range(DC):
                            mm = pe.matmul(ps[0:KTAIL, bank, :], ctxT[:, k, j - 12, P:KEYS], wv[:, k, :],
                                           start=(k == 0), stop=(k == DC - 1))
                    mm.then_inc(s["matmul"], 1)

        @block.vector
        def _(dve):
            dve.memset(kbd[:], 0.0).then_inc(s["zeroed"], 1)
            dve.memset(zero[:], 0.0).then_inc(s["zeroed"], 1)
            dve.wait_ge(s["zeroed"], 2)
            dve.wait_ge(s["ctx_in"], 16 * (B + 2))
            dve.tensor_scalar(tau[:], tau[:], 1.0 / math.sqrt(DK), None, ALU.mult).then_inc(s["scaled"], 1)
            dve.tensor_scalar(delta[:], delta[:], 1.0 / math.sqrt(DK), None, ALU.mult).then_inc(s["scaled"], 1)
            dve.wait_ge(s["scaled"], 2)
            for l in range(2):
                dve.wait_ge(s["w_in"], 64 * (l + 1))
                if l:
                    dve.wait_ge(s["stored"], 16 * (2 + HG) * B)
                for j in range(JOBS):
                    bank = j % 8
                    dve.wait_ge(s["matmul"], JOBS * l + j + 1)
                    if j < 8:
                        n, half = j // 2, j % 2
                        for b in (2 * half, 2 * half + 1):
                            for g in range(HG):
                                r = slice(DK * g, DK * (g + 1))
                                op = dve.tensor_scalar(kbd[r, b, n, g * KEYS:(g + 1) * KEYS],
                                                       ps[r, bank, (b % 2) * KEYS:(b % 2 + 1) * KEYS],
                                                       bk[r, n:n + 1], tau[r, b:b + 1], ALU.add, ALU.mult)
                    elif j < 12:
                        op = dve.tensor_tensor(vm[:, j - 8, :], ps[:, bank, :], bv[:], ALU.add)
                    else:
                        op = dve.tensor_tensor(vt[:, j - 12, :], ps[0:KTAIL, bank, :], bv[0:KTAIL, :], ALU.add)
                    op.then_inc(s["evacuated"], 1)


def token_phase(nc, l, a, scr, c, x_in, x_rows):
    gate = l == 0
    with ExitStack() as ctx:
        def sb(name, shape, dt=F32):
            return ctx.enter_context(nc.sbuf_tensor(f"t{l}_{name}", shape, dt))

        wq, wo = sb("wq", [P, DC, D]), sb("wo", [P, DC, D])
        bq, bo = sb("bq", [P, DC]), sb("bo", [P, D])
        kbd = sb("kbd", [P, GROUPS, HG * KEYS])
        vm, vt = sb("vm", [P, D]), sb("vt", [TROWS, D])
        delta = sb("delta", [P, KEYS])
        x = sb("x", [P, TG, D])
        xbo = sb("xbo", [P, TG, D])
        xn, xnT, qT, oT = (sb(n, [P, TG, D]) for n in ("xn", "xnT", "qT", "oT"))
        xs = sb("xs", [P, TG, D])
        sc = sb("sc", [P, 2, HG, KEYS])
        pr = sb("pr", [P, 2, KEYS, HG])
        pTm, pTt = sb("pTm", [P, 2, HG * P]), sb("pTt", [TROWS, 2, P])
        o = sb("o", [P, 2, D])
        negmax, total = sb("negmax", [P, UNITS, HG]), sb("total", [P, UNITS, HG])
        inv = sb("inv", [P, TG, HEADS])
        stat, mv = sb("stat", [P, 2, TG, 6]), sb("mv", [P, 2, TG, 2])
        ve, rstd = sb("ve", [P, 2, TG]), sb("rstd", [P, 2, TG])
        half, eps, tick = (sb(n, [P, TG]) for n in ("half", "eps", "tick"))
        zT = sb("zT", [P, TG, D])
        if gate:
            z = sb("z", [P, TG, D])
            wg = sb("wg", [P, DC, E])
            top = sb("top", [P, TG, TOPK])
        else:
            z = sb("z", [P, TG, XS])
            xl = sb("xl", [P, TG, D])
            xb2, y = sb("xb2", [P, TG, D]), sb("y", [P, TG, D])
            w1, w2 = sb("w1", [P, DC, LIGHT]), sb("w2", [P, LIGHT // P, D])
            gam, b1, b2 = sb("gam", [P, DC]), sb("b1", [P, LIGHT // P]), sb("b2", [P, D])
            rt = sb("rt", [P, D])
            hT = sb("hT", [P, LIGHT // P, D])
            junk, junk2 = sb("junk", [P, D]), sb("junk2", [P, D])
            ssq, rn, score = sb("ssq", [P, TG]), sb("rn", [P, TG]), sb("score", [P, TG])
        ps = c["ps"]
        s = Sems(nc, ctx, f"t{l}",
                 "w_in kv_in x_in ready x_stored z_stored y_stored "
                 "stats mv ve rstd xn xbo xnT_mm xnT_dve xnT_act q_mm q_out "
                 "scored added negmax exped p_mm pTm pTt pv inv o_out o_mm oT_out proj resid "
                 "z z_mm zT_dve zT_act side_mm side_out top "
                 "ssq ssq_c rn score xb2 h_mm h_out xl")
        block = ctx.enter_context(nc.Block())
        W_IN = (16 * 5 if gate else 16 * 10)

        def turns(engine, body):
            body(0, True, False)
            with engine.Fori(1, NG - 1) as i:
                body(i, False, False)
            body(NG - 1, False, True)

        def load_kv(sp, i):
            b = i // (NG // B)
            for dst, src in ((kbd, "kbd%d" % l), (vm, "vm%d" % l), (vt, "vt%d" % l), (delta, "delta")):
                n = dst[:].shape[0]
                v = scr[src].rearrange("b p n -> (b p) n")[bass.ds(b * n, n), :]
                d = dst[:].rearrange("p g n -> p (g n)") if dst is kbd else dst[:]
                sp.dma_start(d, v).then_inc(s["kv_in"], 16)

        @block.sync
        def _(sp):
            sp.dma_start(x[:], rows(x_in, 0)).then_inc(s["x_in"], 16)
            sp.dma_start(wq[:], a[f"WqT{l}"].rearrange("(k p) n -> p k n", p=P)).then_inc(s["w_in"], 16)
            with nc.allow_non_contiguous_dma(reason="biases by partition"):
                sp.dma_start(bq[:], a[f"bq{l}"].rearrange("(k p) -> p k", p=P)).then_inc(s["w_in"], 16)
                if not gate:
                    sp.dma_start(gam[:], a["light_gamma"].rearrange("(k p) -> p k", p=P)).then_inc(s["w_in"], 16)
                    sp.dma_start(b1[:], a["light_b1"].rearrange("(k p) -> p k", p=P)).then_inc(s["w_in"], 16)
            load_kv(sp, 0)
            sp.dma_start(bo[:], a[f"bo{l}"].partition_broadcast(P)).then_inc(s["w_in"], 16)
            sp.dma_start(wo[:], a[f"WoT{l}"].rearrange("(k p) n -> p k n", p=P)).then_inc(s["w_in"], 16)
            if gate:
                sp.dma_start(wg[:], a["gateT"].rearrange("(k p) n -> p k n", p=P)).then_inc(s["w_in"], 16)
            else:
                sp.dma_start(rt[:], a["routing"].partition_broadcast(P)).then_inc(s["w_in"], 16)
                sp.dma_start(b2[:], a["light_b2"].partition_broadcast(P)).then_inc(s["w_in"], 16)
                sp.dma_start(w1[:], a["light_w1"].rearrange("(k p) n -> p k n", p=P)).then_inc(s["w_in"], 16)
                sp.dma_start(w2[:], a["light_w2"].rearrange("(k p) n -> p k n", p=P)).then_inc(s["w_in"], 16)

            def store_side(i):
                if gate:
                    sp.wait_ge(s["z"], TG * i + TG)
                    sp.dma_start(rows(scr["xw"], i, D), z[:]).then_inc(s["z_stored"], 16)
                else:
                    sp.wait_ge(s["z"], TG * i + TG)
                    sp.wait_ge(s["score"], i + 1)
                    sp.dma_start(rows(scr["xs"], i), z[:]).then_inc(s["z_stored"], 16)
                    sp.wait_ge(s["side_out"], TG * i + TG)
                    sp.dma_start(rows(x_rows, i), y[:]).then_inc(s["y_stored"], 16)

            def turn(i, first, last):
                if not last:
                    sp.wait_ge(s["xbo"], i + 1)
                    sp.wait_ge(s["xn"], TG * i + TG)
                    sp.dma_start(x[:], rows(x_in, i + 1)).then_inc(s["x_in"], 16)
                if not first:
                    store_side(i - 1)
                if not last:
                    sp.wait_ge(s["added"], UNITS * i + UNITS)
                    sp.wait_ge(s["pv"], UNITS * i + UNITS)
                    load_kv(sp, i + 1)
                if gate:
                    sp.wait_ge(s["resid"], TG * i + TG)
                    sp.dma_start(rows(x_rows, i), xs[:]).then_inc(s["x_stored"], 16)

            turns(sp, turn)
            store_side(NG - 1)
            sp.wait_ge(s["z_stored"], 16 * NG)
            sp.wait_ge(s["x_stored" if gate else "y_stored"], 16 * NG)

        @block.gpsimd
        def _(pool):
            pool.memset(half[:], -0.5).then_inc(s["ready"], 1)
            pool.memset(eps[:], EPS).then_inc(s["ready"], 1)
            if not gate:
                pool.memset(z[:], 0.0).then_inc(s["ready"], 1)
            pool.wait_ge(s["ready"], 2 if gate else 3)

            def rstd_of(which, n):
                pool.wait_ge(s["mv"], TG * n + TG)
                pool.tensor_tensor(ve[:, which, :], mv[:, which, :, 1], eps[:], ALU.add).then_inc(s["ve"], 1)
                pool.wait_ge(s["ve"], n + 1)
                pool.tensor_tensor(rstd[:, which, :], ve[:, which, :], half[:], ALU.pow).then_inc(s["rstd"], 1)

            def side(i):
                rstd_of(1, 2 * i + 1 + (i != NG - 1) if isinstance(i, int) else 2 * i + 2)
                if not gate:
                    pool.wait_ge(s["side_out"], TG * i)
                    pool.tensor_tensor(xb2[:], xs[:], b2[:].unsqueeze(1).to_broadcast([P, TG, D]),
                                       ALU.add).then_inc(s["xb2"], 1)
                    pool.wait_ge(s["ssq_c"], i + 1)
                    pool.tensor_tensor(rn[:], ssq[:], half[:], ALU.pow).then_inc(s["rn"], 1)

            rstd_of(0, 0)
            pool.wait_ge(s["w_in"], W_IN)

            def turn(i, first, last):
                if not first:
                    side(i - 1)
                pool.wait_ge(s["x_in"], 16 * i + 16)
                pool.wait_ge(s["resid"], TG * i)
                pool.tensor_tensor(xbo[:], x[:], bo[:].unsqueeze(1).to_broadcast([P, TG, D]),
                                   ALU.add).then_inc(s["xbo"], 1)
                if not last:
                    rstd_of(0, 1 if first else 2 * i + 1)

            turns(pool, turn)
            side(NG - 1)

        @block.vector
        def _(dve):
            def normed(which, n, src, dst, done, base):
                for t in range(TG):
                    dve.bn_stats(stat[:, which, t, :], src[:, t, :]).then_inc(s["stats"], 1)
                dve.wait_ge(s["stats"], TG * n + TG)
                dve.memset(tick[:], 0.0)
                for t in range(TG):
                    dve.bn_aggr(mv[:, which, t, :], stat[:, which, t, :]).then_inc(s["mv"], 1)
                dve.wait_ge(s["rstd"], n + 1)
                for t in range(TG):
                    dve.tensor_scalar(dst[:, t, 0:D], src[:, t, :], mv[:, which, t, 0:1],
                                      rstd[:, which, t:t + 1], ALU.subtract, ALU.mult).then_inc(s[done], 1)

            def side_norm(i):
                n = 2 * i + 1 + (i != NG - 1) if isinstance(i, int) else 2 * i + 2
                if gate:
                    dve.wait_ge(s["z_stored"], 16 * i)
                    dve.wait_ge(s["z_mm"], DC * i)
                    dve.wait_ge(s["resid"], TG * i + TG)
                    normed(1, n, xs, z, "z", 0)
                else:
                    dve.wait_ge(s["resid"], TG * i + TG)
                    normed(1, n, xs, xl, "xl", 0)
                    dve.wait_ge(s["z_stored"], 16 * i)
                    dve.wait_ge(s["z_mm"], DC * i)
                    for t in range(TG):
                        dve.wait_ge(s["xl"], TG * i + t + 1)
                        dve.tensor_tensor_reduce(out=junk[:], in0=xl[:, t, :], in1=rt[:], scale=1.0, scalar=0.0,
                                                 op0=ALU.mult, op1=ALU.add,
                                                 accum_out=score[:, t:t + 1]).then_inc(s["top"], 1)
                        dve.wait_ge(s["top"], TG * i + t + 1)
                    dve.wait_ge(s["ssq"], TG * i + TG)
                    dve.tensor_scalar(ssq[:], ssq[:], 1e-24, None, ALU.max).then_inc(s["ssq_c"], 1)
                    dve.wait_ge(s["rn"], i + 1)
                    for t in range(TG):
                        dve.tensor_scalar(z[:, t, 0:D], xl[:, t, :], rn[:, t:t + 1], math.sqrt(D),
                                          ALU.mult, ALU.mult).then_inc(s["z"], 1)
                    dve.tensor_copy(z[:, :, D], score[:]).then_inc(s["score"], 1)
                    dve.tensor_copy(c["scores"][:, bass.ds(i * TG, TG)], score[:])

            def side_evac(i):
                for k in range(2):
                    dve.wait_ge(s["z_mm"], DC * i + k + 1)
                    if k == 0:
                        dve.wait_ge(s["side_mm"] if gate else s["h_mm"], i if gate else (LIGHT // P) * i)
                    if gate:
                        dve.tensor_copy(zT[:, k, :], ps[:, k, :]).then_inc(s["zT_dve"], 1)
                    else:
                        dve.tensor_scalar(zT[:, k, :], ps[:, k, :], gam[:, k:k + 1], None,
                                          ALU.mult).then_inc(s["zT_dve"], 1)

            def side_out(i):
                if gate:
                    dve.wait_ge(s["side_mm"], i + 1)
                    dve.tensor_copy(c["logits"][:, bass.ds(i * TG * E, TG * E)], ps[:, 4, 0:TG * E])
                    for t in range(TG):
                        op = dve.max(top[:, t, :], ps[:, 4, t * E:(t + 1) * E])
                    op.then_inc(s["top"], 1)
                    dve.wait_ge(s["top"], i + 1)
                    dve.tensor_copy(c["top8"][:, bass.ds(i * TG * TOPK, TG * TOPK)],
                                    top[:].rearrange("p t k -> p (t k)")).then_inc(s["side_out"], 1)
                else:
                    dve.wait_ge(s["xb2"], i + 1)
                    dve.wait_ge(s["y_stored"], 16 * i)
                    for t in range(TG):
                        dve.wait_ge(s["side_mm"], TG * i + t + 1)
                        dve.tensor_tensor(y[:, t, :], ps[:, t, :], xb2[:, t, :], ALU.add).then_inc(s["side_out"], 1)

            dve.wait_ge(s["x_in"], 16)
            normed(0, 0, x, xn, "xn", 0)
            dve.wait_ge(s["w_in"], W_IN)

            def turn(i, first, last):
                for k in range(2):
                    dve.wait_ge(s["xnT_mm"], DC * i + k + 1)
                    dve.tensor_copy(xnT[:, k, :], ps[:, k, :]).then_inc(s["xnT_dve"], 1)
                if not first:
                    side_norm(i - 1)
                    side_evac(i - 1)
                    side_out(i - 1)
                for st in range(UNITS + 4):
                    if st < UNITS:
                        u, bank = st, 2 * (st % 2)
                        dve.wait_ge(s["scored"], UNITS * i + u + 1)
                        if u == 0:
                            dve.wait_ge(s["kv_in"], 64 * i + 64)
                        if u >= 2:
                            dve.wait_ge(s["exped"], UNITS * i + u - 1)
                        dve.tensor_tensor(sc[:, u % 2].rearrange("p (b h) n -> p b h n", b=2),
                                          ps[:, bank:bank + 2, 0:2 * KEYS].rearrange("p b (h n) -> p b h n", h=2),
                                          delta[:].unsqueeze(1).unsqueeze(1).to_broadcast([P, 2, 2, KEYS]),
                                          ALU.add).then_inc(s["added"], 1)
                        dve.wait_ge(s["added"], UNITS * i + u + 1)
                        dve.tensor_reduce(negmax[:, u, :], sc[:, u % 2], AX, ALU.max,
                                          negate=True).then_inc(s["negmax"], 1)
                    if 2 <= st < UNITS + 2:
                        u = st - 2
                        dve.wait_ge(s["p_mm"], UNITS * i + u + 1)
                        if u >= 2:
                            dve.wait_ge(s["pv"], UNITS * i + u - 1)
                        dve.tensor_copy(pTm[:, u % 2, :], ps[:, 4, :]).then_inc(s["pTm"], 1)
                    if st >= 7 and (st - 7) % 4 == 0:
                        t = (st - 7) // 4
                        dve.wait_ge(s["pv"], UNITS * i + GROUPS * (t + 1))
                        dve.reciprocal(inv[:, t, :], total[:, GROUPS * t:GROUPS * (t + 1), :]
                                       .rearrange("p g h -> p (g h)")).then_inc(s["inv"], 1)
                        dve.wait_ge(s["inv"], TG * i + t + 1)
                        if t >= 2:
                            dve.wait_ge(s["o_mm"], TG * i + t - 1)
                        dve.tensor_tensor(o[:, t % 2, :].rearrange("p (h d) -> p h d", d=DK),
                                          ps[:, 6 + t % 2, :].rearrange("p (h d) -> p h d", d=DK),
                                          inv[:, t, :].unsqueeze(2).to_broadcast([P, HEADS, DK]),
                                          ALU.mult).then_inc(s["o_out"], 1)
                if not last:
                    dve.wait_ge(s["x_in"], 16 * i + 32)
                    dve.wait_ge(s["xnT_mm"], DC * i + DC)
                    normed(0, 1 if first else 2 * i + 1, x, xn, "xn", 0)
                dve.wait_ge(s["xbo"], i + 1)
                if gate:
                    dve.wait_ge(s["x_stored"], 16 * i)
                elif not first:
                    dve.wait_ge(s["xb2"], i)
                for t in range(TG):
                    dve.wait_ge(s["proj"], TG * i + t + 1)
                    dve.tensor_tensor(xs[:, t, :], ps[:, t, :], xbo[:, t, :], ALU.add).then_inc(s["resid"], 1)

            turns(dve, turn)
            side_norm(NG - 1)
            side_evac(NG - 1)
            side_out(NG - 1)

        @block.scalar
        def _(act):
            act.wait_ge(s["w_in"], W_IN)

            def side_norm(i):
                if not gate:
                    act.wait_ge(s["rn"], i)
                    for t in range(TG):
                        act.wait_ge(s["xl"], TG * i + t + 1)
                        act.activation(junk2[:], xl[:, t, :], ACT.Square,
                                       accum_out=ssq[:, t:t + 1]).then_inc(s["ssq"], 1)
                        act.wait_ge(s["ssq"], TG * i + t + 1)

            def side_evac(i):
                for k in range(2, DC):
                    act.wait_ge(s["z_mm"], DC * i + k + 1)
                    if k == 2:
                        act.wait_ge(s["side_mm"] if gate else s["h_mm"], i if gate else (LIGHT // P) * i)
                    if gate:
                        act.copy(zT[:, k, :], ps[:, k, :]).then_inc(s["zT_act"], 1)
                    else:
                        act.activation(zT[:, k, :], ps[:, k, :], ACT.Copy,
                                       scale=gam[:, k:k + 1]).then_inc(s["zT_act"], 1)
                if not gate:
                    for f in range(LIGHT // P):
                        act.wait_ge(s["h_mm"], (LIGHT // P) * i + f + 1)
                        if f == 0:
                            act.wait_ge(s["side_mm"], TG * i)
                        act.activation(hT[:, f, :], ps[:, 4 + f, :], ACT.Gelu,
                                       bias=b1[:, f:f + 1]).then_inc(s["h_out"], 1)

            def turn(i, first, last):
                for k in range(2, DC):
                    act.wait_ge(s["xnT_mm"], DC * i + k + 1)
                    act.copy(xnT[:, k, :], ps[:, k, :]).then_inc(s["xnT_act"], 1)
                for n in range(DC):
                    act.wait_ge(s["q_mm"], DC * i + n + 1)
                    act.activation(qT[:, n, :], ps[:, 4 + n, :], ACT.Identity,
                                   bias=bq[:, n:n + 1]).then_inc(s["q_out"], 1)
                if not first:
                    side_norm(i - 1)
                    side_evac(i - 1)
                for st in range(UNITS + 5):
                    if st < UNITS:
                        u = st
                        act.wait_ge(s["negmax"], UNITS * i + u + 1)
                        if u >= 2:
                            act.wait_ge(s["p_mm"], UNITS * i + u - 1)
                        for h in range(HG):
                            op = act.activation(pr[:, u % 2, :, h], sc[:, u % 2, h, :], ACT.Exp,
                                                bias=negmax[:, u, h:h + 1], accum_out=total[:, u, h:h + 1])
                        op.then_inc(s["exped"], 1)
                    if 2 <= st < UNITS + 2:
                        u = st - 2
                        act.wait_ge(s["p_mm"], UNITS * i + u + 1)
                        if u >= 2:
                            act.wait_ge(s["pv"], UNITS * i + u - 1)
                        act.copy(pTt[:, u % 2, :], ps[0:TROWS, 5, 0:P]).then_inc(s["pTt"], 1)
                    if st >= 8 and (st - 8) % 4 == 0:
                        t = (st - 8) // 4
                        act.wait_ge(s["o_mm"], TG * i + t + 1)
                        act.copy(oT[:, :, t * P:(t + 1) * P],
                                 ps[:, 6 + t % 2, :].rearrange("p (k n) -> p k n", k=DC)).then_inc(s["oT_out"], 1)

            turns(act, turn)
            side_norm(NG - 1)
            side_evac(NG - 1)

        @block.tensor
        def _(pe):
            ident = c["ident"]
            pe.wait_ge(s["w_in"], W_IN)

            def transposes(src, banks_done):
                for k in range(DC):
                    for t in range(TG):
                        mm = pe.transpose(ps[:, k, t * P:(t + 1) * P], src[:, t, k * P:(k + 1) * P], ident[:])
                    mm.then_inc(banks_done, 1)

            def side(i):
                pe.wait_ge(s["z"], TG * i + TG)
                transposes(z, s["z_mm"])
                pe.wait_ge(s["zT_dve"], 2 * i + 2)
                pe.wait_ge(s["zT_act"], 2 * i + 2)
                if gate:
                    for t in range(TG):
                        for k in range(DC):
                            mm = pe.matmul(ps[:, 4, t * E:(t + 1) * E], zT[:, k, t * P:(t + 1) * P], wg[:, k, :],
                                           start=(k == 0), stop=(k == DC - 1))
                    mm.then_inc(s["side_mm"], 1)
                else:
                    for f in range(LIGHT // P):
                        for k in range(DC):
                            mm = pe.matmul(ps[:, 4 + f, :], w1[:, k, f * P:(f + 1) * P], zT[:, k, :],
                                           start=(k == 0), stop=(k == DC - 1))
                        mm.then_inc(s["h_mm"], 1)
                    pe.wait_ge(s["h_out"], (LIGHT // P) * (i + 1))
                    for t in range(TG):
                        for f in range(LIGHT // P):
                            mm = pe.matmul(ps[:, t, :], hT[:, f, t * P:(t + 1) * P], w2[:, f, :],
                                           start=(f == 0), stop=(f == LIGHT // P - 1))
                        mm.then_inc(s["side_mm"], 1)

            def scores(i, u):
                t, g, bank = u // GROUPS, u % GROUPS, 2 * (u % 2)
                if u >= 2:
                    pe.wait_ge(s["added"], UNITS * i + u - 1)
                for hh in range(2):
                    mm = pe.matmul(ps[:, bank + hh, 0:2 * KEYS], qT[:, g, t * P:(t + 1) * P],
                                   kbd[:, g, hh * 2 * KEYS:(hh + 1) * 2 * KEYS], start=True, stop=True)
                mm.then_inc(s["scored"], 1)

            def p_transposes(i, u):
                pe.wait_ge(s["exped"], UNITS * i + u + 1)
                if u >= 1:
                    pe.wait_ge(s["pTm"], UNITS * i + u)
                    pe.wait_ge(s["pTt"], UNITS * i + u)
                for h in range(HG):
                    pe.transpose(ps[:, 4, h * P:(h + 1) * P], pr[:, u % 2, 0:P, h], ident[:])
                pe.transpose(ps[0:TROWS, 5, 0:P], pr[:, u % 2, P:KEYS, :].rearrange("p n h -> p (n h)"),
                             ident[:]).then_inc(s["p_mm"], 1)

            def values(i, u):
                t, g = u // GROUPS, u % GROUPS
                pe.wait_ge(s["pTm"], UNITS * i + u + 1)
                pe.wait_ge(s["pTt"], UNITS * i + u + 1)
                if g == 0 and t >= 2:
                    pe.wait_ge(s["oT_out"], TG * i + t - 1)
                bank = 6 + t % 2
                pe.matmul(ps[:, bank, g * P:(g + 1) * P], pTt[:, u % 2, :], vt[:, g * P:(g + 1) * P],
                          start=True, stop=False, skip_group_check=True)
                for h in range(HG):
                    cols = slice(g * P + h * DK, g * P + (h + 1) * DK)
                    mm = pe.matmul(ps[:, bank, cols], pTm[:, u % 2, h * P:(h + 1) * P], vm[:, cols],
                                   start=False, stop=True, skip_group_check=True)
                mm.then_inc(s["pv"], 1)

            def o_transposes(i, t):
                pe.wait_ge(s["o_out"], TG * i + t + 1)
                for k in range(DC):
                    mm = pe.transpose(ps[:, 6 + t % 2, k * P:(k + 1) * P], o[:, t % 2, k * P:(k + 1) * P], ident[:])
                mm.then_inc(s["o_mm"], 1)

            def project(i, t):
                pe.wait_ge(s["oT_out"], TG * i + t + 1)
                for k in range(DC):
                    mm = pe.matmul(ps[:, t, :], oT[:, k, t * P:(t + 1) * P], wo[:, k, :],
                                   start=(k == 0), stop=(k == DC - 1))
                mm.then_inc(s["proj"], 1)

            def turn(i, first, last):
                pe.wait_ge(s["xn"], TG * i + TG)
                pe.wait_ge(s["resid"], TG * i)
                transposes(xn, s["xnT_mm"])
                pe.wait_ge(s["xnT_dve"], 2 * i + 2)
                pe.wait_ge(s["xnT_act"], 2 * i + 2)
                for n in range(DC):
                    for k in range(DC):
                        mm = pe.matmul(ps[:, 4 + n, :], wq[:, k, n * P:(n + 1) * P], xnT[:, k, :],
                                       start=(k == 0), stop=(k == DC - 1))
                    mm.then_inc(s["q_mm"], 1)
                if not first:
                    pe.wait_ge(s["q_out"], DC * i + 2)
                    side(i - 1)
                    pe.wait_ge(s["side_out"], i if gate else TG * i)
                pe.wait_ge(s["q_out"], DC * i + DC)
                pe.wait_ge(s["kv_in"], 64 * i + 64)
                for st in range(UNITS + 4):
                    if st < UNITS:
                        scores(i, st)
                    if 2 <= st < UNITS + 2:
                        p_transposes(i, st - 2)
                    if 3 <= st < UNITS + 3:
                        values(i, st - 3)
                    if st >= 8 and st % 4 == 0:
                        o_transposes(i, st // 4 - 2)
                pe.wait_ge(s["added"], UNITS * i + UNITS)
                project(i, 0)
                project(i, 1)
                o_transposes(i, 3)
                project(i, 2)
                project(i, 3)

            turns(pe, turn)
            pe.wait_ge(s["resid"], TG * NG)
            side(NG - 1)


def expert_slots_phase(nc, a, scr, c):
    BIG = 65536.0
    W = P + 2
    with ExitStack() as ctx:
        def sb(name, shape, dt=F32):
            return ctx.enter_context(nc.sbuf_tensor(f"r_{name}", shape, dt))

        prob, gt, eq, run = (sb(n, [P, NT, E]) for n in ("prob", "gt", "eq", "run"))
        restart = sb("restart", [P, NT, E])
        edge, z, rz, need, ws = (sb(n, [P, NT]) for n in ("edge", "z", "rz", "need", "ws"))
        selT, count = sb("selT", [NT, E, P]), sb("count", [NT, E, P])
        restartT = sb("restartT", [NT, E, P])
        before = sb("before", [NT, NT + 1])
        base, upto = sb("base", [NT + 1, E]), sb("upto", [NT + 1, E])
        table = sb("table", [NT + 1, E, W])
        slots = sb("slots", [NT + 1, CAP])
        ge, hot = sb("ge", [NT + 1, 2, CAP]), sb("hot", [NT + 1, 2, CAP])
        slot_no = sb("slot_no", [P, CC])
        junk = sb("junk", [P, CC, P])
        rank = sb("rank", [P, E, CC])
        found = sb("found", [P, E, CC, 2])
        zero = sb("zero", [P, CC, XW])
        ps = c["ps"]
        s = Sems(nc, ctx, "r", "made shifted exped step weights selected selT_mm counted based tabled "
                               "ge_made hot_made hot_mm looked_up stored")
        block = ctx.enter_context(nc.Block())

        @block.gpsimd
        def _(pool):
            pool.memset(before[:], 1.0).then_inc(s["made"], 1)
            pool.wait_ge(s["made"], 1)
            pool.affine_select(out=before[:], in_=before[:], compare_op=ALU.is_gt, fill=0.0, base=0,
                               pattern=[[1, NT + 1]], channel_multiplier=-1).then_inc(s["made"], 1)
            pool.iota(slots[:], [[1, CAP]], base=0, channel_multiplier=0,
                      allow_small_or_imprecise_dtypes=True).then_inc(s["made"], 1)
            pool.iota(slot_no[:], [[P, CC]], base=0, channel_multiplier=1,
                      allow_small_or_imprecise_dtypes=True).then_inc(s["made"], 1)
            pool.iota(table[:, :, P], [[0, E]], base=0, channel_multiplier=P,
                      allow_small_or_imprecise_dtypes=True).then_inc(s["made"], 1)
            pool.memset(table[:, :, P + 1], 0.0).then_inc(s["made"], 1)
            pool.wait_ge(s["made"], 6)
            pool.memset(zero[:], 0.0).then_inc(s["made"], 1)
            pool.wait_ge(s["made"], 7)
            pool.memset(table[NT:NT + 1, :, P + 1], 1.0).then_inc(s["made"], 1)
            pool.wait_ge(s["made"], 8)
            pool.memset(table[NT:NT + 1, :, 0:P], BIG).then_inc(s["made"], 1)

        @block.sync
        def _(sp):
            sp.wait_ge(s["made"], 9)
            sp.dma_start(scr["xw"][NTOK:NTOK + CAP, :].rearrange("(c p) d -> p c d", p=P),
                         zero[:]).then_inc(s["stored"], 16)
            sp.dma_start(scr["x1"][NTOK:NTOK + CAP, :].rearrange("(c p) d -> p c d", p=P),
                         zero[:, :, 0:D]).then_inc(s["stored"], 16)
            sp.wait_ge(s["weights"], 1)
            sp.dma_start(scr["xw"][0:NTOK, D:XW].rearrange("(t p) e -> p t e", p=P),
                         prob[:]).then_inc(s["stored"], 16)
            sp.wait_ge(s["stored"], 48)

        @block.scalar
        def _(act):
            act.wait_ge(s["shifted"], 1)
            act.activation(prob[:], prob[:], ACT.Exp).then_inc(s["exped"], 1)
            act.activation(edge[:], edge[:], ACT.Exp).then_inc(s["exped"], 1)

        @block.vector
        def _(dve):
            steps = [0]

            def link(op):
                steps[0] += 1
                op.then_inc(s["step"], 1)
                dve.wait_ge(s["step"], steps[0])

            def by_tile(v):
                return v[:].unsqueeze(2).to_broadcast([P, NT, E])

            logits = c["logits"][:].rearrange("p (t e) -> p t e", e=E)
            top8 = c["top8"][:].rearrange("p (t k) -> p t k", k=TOPK)
            dve.memset(restart[:], 1.0)
            dve.memset(restartT[:], 1.0)
            dve.tensor_tensor(edge[:], top8[:, :, TOPK - 1], top8[:, :, 0], ALU.subtract).then_inc(s["step"], 1)
            link(dve.memset(upto[:], 2 * BIG))
            steps[0] += 1
            dve.wait_ge(s["step"], steps[0])
            dve.tensor_tensor(prob[:], logits, top8[:, :, 0].unsqueeze(2).to_broadcast([P, NT, E]),
                              ALU.subtract).then_inc(s["shifted"], 1)
            link(dve.memset(restart[:, :, 0:1], 0.0))
            link(dve.memset(restartT[:, :, 0:1], 0.0))
            dve.wait_ge(s["exped"], 2)
            link(dve.tensor_reduce(z[:], prob[:], AX, ALU.add))
            link(dve.reciprocal(rz[:], z[:]))
            link(dve.tensor_tensor(prob[:], prob[:], by_tile(rz), ALU.mult))
            link(dve.tensor_tensor(edge[:], edge[:], rz[:], ALU.mult))
            link(dve.tensor_tensor(gt[:], prob[:], by_tile(edge), ALU.is_gt))
            link(dve.tensor_tensor(eq[:], prob[:], by_tile(edge), ALU.is_equal))
            link(dve.tensor_reduce(z[:], gt[:], AX, ALU.add))
            link(dve.tensor_scalar(need[:], z[:], -1.0, float(TOPK), ALU.mult, ALU.add))
            link(dve.tensor_tensor_scan(run[:].rearrange("p t e -> p (t e)"),
                                        restart[:].rearrange("p t e -> p (t e)"),
                                        eq[:].rearrange("p t e -> p (t e)"), 0.0, ALU.mult, ALU.add))
            link(dve.tensor_tensor(run[:], run[:], by_tile(need), ALU.is_le))
            link(dve.tensor_tensor(eq[:], run[:], eq[:], ALU.mult))
            dve.tensor_tensor(gt[:], gt[:], eq[:], ALU.add).then_inc(s["selected"], 1)
            dve.wait_ge(s["selected"], 1)
            link(dve.tensor_tensor(prob[:], prob[:], gt[:], ALU.mult))
            link(dve.tensor_reduce(ws[:], prob[:], AX, ALU.add))
            link(dve.reciprocal(ws[:], ws[:]))
            dve.tensor_tensor(prob[:], prob[:], by_tile(ws), ALU.mult).then_inc(s["weights"], 1)
            for b in range(8):
                dve.wait_ge(s["selT_mm"], b + 1)
                op = dve.tensor_copy(selT[:, 4 * b:4 * b + 4, :].rearrange("p e n -> p (e n)"), ps[0:NT, b, :])
                op.then_inc(s["step"], 1)
            steps[0] += 8
            dve.wait_ge(s["step"], steps[0])
            dve.tensor_tensor_scan(count[:].rearrange("p e n -> p (e n)"),
                                   restartT[:].rearrange("p e n -> p (e n)"),
                                   selT[:].rearrange("p e n -> p (e n)"), 0.0, ALU.mult,
                                   ALU.add).then_inc(s["counted"], 1)
            dve.wait_ge(s["based"], 1)
            link(dve.tensor_copy(base[:], ps[0:NT + 1, 0, 0:E]))
            link(dve.tensor_tensor(upto[0:NT, :], base[0:NT, :], count[:, :, P - 1], ALU.add))
            dve.wait_ge(s["made"], 9)
            dve.tensor_tensor(table[0:NT, :, 0:P], count[:], base[0:NT, :].unsqueeze(2).to_broadcast([NT, E, P]),
                              ALU.add).then_inc(s["tabled"], 1)

            def one_hot(e, q):
                dve.tensor_scalar(ge[:, q, :], slots[:], base[:, bass.ds(e, 1)], None,
                                  ALU.is_ge).then_inc(s["ge_made"], 1)
                dve.wait_ge(s["ge_made"], e + 1)
                dve.scalar_tensor_tensor(hot[:, q, :], slots[:], upto[:, bass.ds(e, 1)], ge[:, q, :],
                                         ALU.is_lt, ALU.mult).then_inc(s["hot_made"], 1)

            def look_up(e, q):
                dve.wait_ge(s["hot_mm"], e + 1)
                dve.wait_ge(s["looked_up"], e)
                for n in range(CC):
                    bank, at = 2 * q + n // 2, (n % 2) * W
                    dve.tensor_scalar(junk[:, n, :], ps[:, bank, at:at + P], slot_no[:, n:n + 1], 0.0, ALU.is_le, ALU.add,
                                      accum_out=rank[:, bass.ds(e, 1), n])
                dve.tensor_copy(
                    found[:, bass.ds(e, 1), :, :].rearrange("p o (b n) w -> p (o b) n w", b=2),
                    ps[:, 2 * q:2 * q + 2, 0:2 * W].rearrange("p b (n w) -> p b n w", w=W)[:, :, :, P:W],
                ).then_inc(s["looked_up"], 1)

            one_hot(0, 0)
            with dve.Fori(0, E // 2 - 1) as j:
                one_hot(2 * j + 1, 1)
                look_up(2 * j, 0)
                one_hot(2 * j + 2, 0)
                look_up(2 * j + 1, 1)
            one_hot(E - 1, 1)
            look_up(E - 2, 0)
            look_up(E - 1, 1)
            dve.wait_ge(s["looked_up"], E)
            link(dve.tensor_tensor(rank[:], rank[:], found[:, :, :, 0], ALU.add))
            link(dve.tensor_tensor(found[:, :, :, 1], found[:, :, :, 1],
                                   slot_no[:].unsqueeze(1).to_broadcast([P, E, CC]), ALU.mult))
            link(dve.tensor_tensor(rank[:], rank[:], found[:, :, :, 1], ALU.add))
            dve.tensor_copy(c["expert_rows"][:].rearrange("p (e n) -> p e n", n=CC), rank[:])

        @block.tensor
        def _(pe):
            pe.wait_ge(s["selected"], 1)
            for e in range(E):
                mm = pe.transpose(ps[0:NT, e // 4, (e % 4) * P:(e % 4 + 1) * P], gt[:, :, e], c["ident"][:])
                if e % 4 == 3:
                    mm.then_inc(s["selT_mm"], 1)
            pe.wait_ge(s["counted"], 1)
            pe.wait_ge(s["made"], 9)
            pe.matmul(ps[0:NT + 1, 0, 0:E], before[:], count[:, :, P - 1], start=True,
                      stop=True).then_inc(s["based"], 1)
            pe.wait_ge(s["tabled"], 1)

            def look_up(e, q, first):
                pe.wait_ge(s["hot_made"], e + 1)
                if not first:
                    pe.wait_ge(s["looked_up"], e - 1)
                for n in range(CC):
                    bank, at = 2 * q + n // 2, (n % 2) * W
                    mm = pe.matmul(ps[:, bank, at:at + W], hot[:, q, n * P:(n + 1) * P],
                                   table[:, bass.ds(e, 1), :].rearrange("p o w -> p (o w)"), start=True, stop=True)
                mm.then_inc(s["hot_mm"], 1)

            look_up(0, 0, True)
            look_up(1, 1, True)
            with pe.Fori(1, E // 2) as j:
                look_up(2 * j, 0, False)
                look_up(2 * j + 1, 1, False)


def expert_phase(nc, a, scr, c):
    with ExitStack() as ctx:
        def sb(name, shape, dt=F32):
            return ctx.enter_context(nc.sbuf_tensor(f"e_{name}", shape, dt))

        wgu = [sb(f"wgu{q}", [P, DC, 2 * F]) for q in range(2)]
        wd = [sb(f"wd{q}", [P, FC, D]) for q in range(2)]
        idx = [sb(f"idx{q}", [P, CC], I32) for q in range(2)]
        xe = [sb(f"xe{q}", [P, CC, XW]) for q in range(2)]
        xT = [sb(f"xT{q}", [P, DC, CAP]) for q in range(2)]
        weight = [sb(f"weight{q}", [P, CC]) for q in range(2)]
        y = [sb(f"y{q}", [P, CC, D]) for q in range(2)]
        sig = sb("sig", [P, 2, CAP])
        hT = sb("hT", [P, FC, CAP])
        one, tick = sb("one", [P, 1]), sb("tick", [P, 2, CC + 1])
        ps = c["ps"]
        s = Sems(nc, ctx, "e", "ready w_in0 w_in1 idx gathered0 gathered1 scattered x_mm xT_dve xT_act weight gu_mm silu h d_mm y")
        block = ctx.enter_context(nc.Block())

        def turns(engine, body):
            body(0, True, False)
            with engine.Fori(1, E // 2 - 1) as j:
                body(j, False, False)
            body(E // 2 - 1, False, True)

        def arrivals(e, q):
            return (e - q) // 2 + 1

        @block.sync
        def _(sp):
            def load(e, q):
                sp.dma_start(wgu[q][:], a["gate_upT"][bass.ds(e * D, D), :]
                             .rearrange("(k p) f -> p k f", p=P)).then_inc(s[f"w_in{q}"], 16)
                sp.dma_start(wd[q][:], a["downT"][bass.ds(e * F, F), :]
                             .rearrange("(k p) d -> p k d", p=P)).then_inc(s[f"w_in{q}"], 16)

            load(0, 0)
            load(1, 1)

            def turn(j, first, last):
                if not last:
                    for q in range(2):
                        sp.wait_ge(s["d_mm"], CC * (2 * j + q) + CC)
                        load(2 * j + q + 2, q)

            turns(sp, turn)

        @block.gpsimd
        def _(pool):
            pool.memset(one[:], 1.0).then_inc(s["ready"], 1)
            pool.wait_ge(s["ready"], 1)

            def stand(q, n):
                pool.tensor_tensor(tick[:, q, n:n + 1], one[:], one[:], ALU.add)

            def gather(e, q, first):
                if not first:
                    pool.wait_ge(s["scattered"], 16 * CC * (e - 1))
                    pool.wait_ge(s["x_mm"], DC * (e - 1))
                    pool.wait_ge(s["weight"], e - 1)
                pool.tensor_copy(idx[q][:], c["expert_rows"][:, bass.ds(CC * e, CC)]).then_inc(s["idx"], 1)
                pool.wait_ge(s["idx"], e + 1)
                stand(q, CC)
                for n in range(CC):
                    pool.indirect_dma_start(
                        out=xe[q][:, n, :], out_offset=None, in_=scr["xw"][:, :],
                        in_offset=bass.IndirectOffsetOnAxis(ap=idx[q][:, n:n + 1], axis=0),
                    ).then_inc(s[f"gathered{q}"], 16)

            def scatter(e, q):
                pool.wait_ge(s["scattered"], 16 * CC * e)
                for n in range(CC):
                    pool.wait_ge(s["y"], CC * e + n + 1)
                    stand(q, n)
                    pool.indirect_dma_start(
                        out=scr["x1"][:, :], out_offset=bass.IndirectOffsetOnAxis(ap=idx[q][:, n:n + 1], axis=0),
                        in_=y[q][:, n, :], in_offset=None, compute_op=ALU.add).then_inc(s["scattered"], 16)

            gather(0, 0, True)

            def turn(j, first, last):
                gather(2 * j + 1, 1, first)
                scatter(2 * j, 0)
                if not last:
                    gather(2 * j + 2, 0, False)
                scatter(2 * j + 1, 1)

            turns(pool, turn)
            pool.wait_ge(s["scattered"], 16 * CC * E)

        @block.vector
        def _(dve):
            def xT_half(e, q):
                for k in (0, 2):
                    dve.wait_ge(s["x_mm"], DC * e + k + 1)
                    dve.tensor_copy(xT[q][:, k, :], ps[:, 4, :]).then_inc(s["xT_dve"], 1)
                dve.wait_ge(s[f"gathered{q}"], arrivals(e, q) * 16 * CC)
                dve.tensor_scalar(weight[q][:].unsqueeze(2), xe[q][:, :, bass.ds(D + e, 1)], 1.0, None,
                                  ALU.mult).then_inc(s["weight"], 1)

            xT_half(0, 0)

            def expert(e, q, first, last):
                for f in range(FC):
                    b = 2 * ((FC * q + f) % 2)
                    dve.wait_ge(s["silu"], FC * e + f + 1)
                    dve.tensor_tensor(hT[:, f, :], sig[:, (FC * q + f) % 2, :], ps[:, b + 1, :],
                                      ALU.mult).then_inc(s["h"], 1)
                if not last:
                    xT_half(e + 1, 1 - q)
                if not first:
                    dve.wait_ge(s["scattered"], 16 * CC * (e - 1))
                dve.wait_ge(s["weight"], e + 1)
                for n in range(CC):
                    dve.wait_ge(s["d_mm"], CC * e + n + 1)
                    dve.tensor_scalar(y[q][:, n, :], ps[:, 6 + n % 2, :], weight[q][:, n:n + 1], None,
                                      ALU.mult).then_inc(s["y"], 1)

            def turn(j, first, last):
                expert(2 * j, 0, first, False)
                expert(2 * j + 1, 1, first, last)

            turns(dve, turn)

        @block.scalar
        def _(act):
            def xT_half(e, q):
                for k in (1, 3):
                    act.wait_ge(s["x_mm"], DC * e + k + 1)
                    act.copy(xT[q][:, k, :], ps[:, 5, :]).then_inc(s["xT_act"], 1)

            xT_half(0, 0)

            def expert(e, q, first, last):
                for f in range(FC):
                    b = 2 * ((FC * q + f) % 2)
                    act.wait_ge(s["gu_mm"], FC * e + f + 1)
                    if not (first and q == 0 and f < 2):
                        act.wait_ge(s["h"], FC * e + f - 1)
                    act.activation(sig[:, (FC * q + f) % 2, :], ps[:, b, :], ACT.Silu).then_inc(s["silu"], 1)
                if not last:
                    xT_half(e + 1, 1 - q)

            def turn(j, first, last):
                expert(2 * j, 0, first, False)
                expert(2 * j + 1, 1, first, last)

            turns(act, turn)

        @block.tensor
        def _(pe):
            def transposes(e, q, start):
                pe.wait_ge(s[f"gathered{q}"], arrivals(e, q) * 16 * CC)
                for k in range(DC):
                    if not (start and k < 2):
                        pe.wait_ge(s["xT_dve" if k % 2 == 0 else "xT_act"], 2 * e + k // 2)
                    for n in range(CC):
                        mm = pe.transpose(ps[:, 4 + k % 2, n * P:(n + 1) * P],
                                          xe[q][:, n, k * P:(k + 1) * P], c["ident"][:])
                    mm.then_inc(s["x_mm"], 1)

            transposes(0, 0, True)

            def expert(e, q, first, last):
                pe.wait_ge(s[f"w_in{q}"], arrivals(e, q) * 32)
                pe.wait_ge(s["xT_dve"], 2 * e + 2)
                pe.wait_ge(s["xT_act"], 2 * e + 2)
                for f in range(FC):
                    b = 2 * ((FC * q + f) % 2)
                    if not (first and q == 0 and f < 2):
                        pe.wait_ge(s["h"], FC * e + f - 1)
                    for part in range(2):
                        for k in range(DC):
                            col = part * F + f * P
                            mm = pe.matmul(ps[:, b + part, :], wgu[q][:, k, col:col + P], xT[q][:, k, :],
                                           start=(k == 0), stop=(k == DC - 1))
                    mm.then_inc(s["gu_mm"], 1)
                if not last:
                    transposes(e + 1, 1 - q, False)
                pe.wait_ge(s["h"], FC * e + FC)
                for n in range(CC):
                    if not (first and q == 0 and n < 2):
                        pe.wait_ge(s["y"], CC * e + n - 1)
                    for f in range(FC):
                        mm = pe.matmul(ps[:, 6 + n % 2, :], hT[:, f, n * P:(n + 1) * P], wd[q][:, f, :],
                                       start=(f == 0), stop=(f == FC - 1))
                    mm.then_inc(s["d_mm"], 1)

            def turn(j, first, last):
                expert(2 * j, 0, first, False)
                expert(2 * j + 1, 1, first, last)

            turns(pe, turn)


def routing_phase(nc, a, scr, c):
    R = P // B
    C = SEQ // R
    LOGK = math.log(EFF_K)
    MADE = 3 + 3 * B + 4
    with ExitStack() as ctx:
        def sb(name, shape, dt=F32):
            return ctx.enter_context(nc.sbuf_tensor(f"d_{name}", shape, dt))

        flat = sb("flat", [NT, P])
        sco, sbv, ex = sb("sco", [P, C]), sb("sbv", [P, C]), sb("ex", [P, C])
        top, wide, wideT, smax = sb("top", [P, 1]), sb("wide", [P, R]), sb("wideT", [P, R]), sb("smax", [P, 1])
        na, nm, part, lse = (sb(n, [P, 1]) for n in ("na", "nm", "part", "lse"))
        same, earlier, ones = sb("same", [P, P]), sb("earlier", [P, P]), sb("ones", [P, C])
        pick = sb("pick", [P, B, P])
        u, below, equal, run, sel, pos = (sb(n, [P, C]) for n in ("u", "below", "equal", "run", "sel", "pos"))
        edge, bit, cand, few = (sb(n, [P, 1], I32) for n in ("edge", "bit", "cand", "few"))
        cnt, need, pre = (sb(n, [P, 1]) for n in ("cnt", "need", "pre"))
        batch = sb("batch", [P, B])
        row, col = sb("row", [P, 1]), sb("col", [P, C])
        vals = sb("vals", [P, C, 2 * B], BF16)
        slots = sb("slots", [P, ROUTED])
        hot = sb("hot", [P, 4, ROUTED], BF16)
        found, rows_f = sb("found", [2 * B, ROUTED]), sb("rows_f", [P, B, CC])
        ps = c["ps"]
        s = Sems(nc, ctx, "d", "w_in made flat_mm flat flat_out s_in step ready shifted exped summed logged na "
                               "cand counted count_mm shift edge pre_mm hot hot_mm found found_mm")
        block = ctx.enter_context(nc.Block())

        @block.sync
        def _(sp):
            sp.dma_start(c["hw1"][:], a["heavy_w1"].rearrange("(k p) f -> p k f", p=P)).then_inc(c["hw_in"], 16)
            sp.wait_ge(s["flat"], 1)
            sp.dma_start(scr["scores"].rearrange("(t p) -> t p", p=P), flat[:]).then_inc(s["flat_out"], 16)
            sp.wait_ge(s["flat_out"], 16)
            sp.dma_start(sco[:], scr["scores"].rearrange("(q j) -> q j", j=C)).then_inc(s["s_in"], 16)
            sp.dma_start(c["hw2"][:], a["heavy_w2"].rearrange("(f p) d -> p f d", p=P)).then_inc(c["hw_in"], 16)
            sp.dma_start(c["hb2"][:], a["heavy_b2"].partition_broadcast(P)).then_inc(c["hw_in"], 16)
            with nc.allow_non_contiguous_dma(reason="biases and scales by partition"):
                sp.dma_start(c["hb1"][:], a["heavy_b1"].rearrange("(k p) -> p k", p=P)).then_inc(c["hw_in"], 16)
                sp.dma_start(c["hgam"][:], a["heavy_gamma"].rearrange("(k p) -> p k", p=P)).then_inc(c["hw_in"], 16)

        @block.gpsimd
        def _(pool):
            n = [0]

            def made(op):
                n[0] += 1
                op.then_inc(s["made"], 1)
                pool.wait_ge(s["made"], n[0])

            made(pool.memset(same[:], 0.0))
            made(pool.memset(batch[:], 0.0))
            made(pool.memset(pick[:], 0.0))
            for b in range(B):
                made(pool.memset(same[R * b:R * (b + 1), R * b:R * (b + 1)], 1.0))
                made(pool.memset(batch[R * b:R * (b + 1), b:b + 1], 1.0))
                made(pool.memset(pick[R * b:R * b + 1, b, :], 1.0))
            made(pool.affine_select(out=earlier[:], in_=same[:], compare_op=ALU.is_gt, fill=0.0, base=0,
                                    pattern=[[1, P]], channel_multiplier=-1))
            made(pool.iota(row[:], [[0, 1]], base=0, channel_multiplier=1, allow_small_or_imprecise_dtypes=True))
            made(pool.iota(col[:], [[1, C]], base=0, channel_multiplier=0, allow_small_or_imprecise_dtypes=True))
            made(pool.iota(slots[:], [[1, ROUTED]], base=0, channel_multiplier=0,
                           allow_small_or_imprecise_dtypes=True))
            assert n[0] == MADE


        @block.scalar
        def _(act):
            def turn(i):
                act.wait_ge(s["shifted"], i + 1)
                act.activation(ex[:], sbv[:], ACT.Exp, bias=nm[:], accum_out=part[:]).then_inc(s["exped"], 1)
                act.wait_ge(s["summed"], i + 1)
                act.activation(lse[:], ps[:, 1, 0:1], ACT.Ln).then_inc(s["logged"], 1)

            with act.Fori(0, ITERS - 1) as i:
                turn(i)

        @block.tensor
        def _(pe):
            pe.transpose(ps[0:NT, 0, 0:P], c["scores"][:], c["ident"][:]).then_inc(s["flat_mm"], 1)
            pe.wait_ge(s["made"], MADE)
            with pe.Fori(0, ITERS - 1) as i:
                pe.wait_ge(s["exped"], i + 1)
                pe.matmul(ps[:, 1, 0:1], same[:], part[:], start=True, stop=True).then_inc(s["summed"], 1)
            with pe.Fori(0, 31) as i:
                pe.wait_ge(s["counted"], i + 1)
                pe.matmul(ps[:, 2, 0:1], same[:], cnt[:], start=True, stop=True).then_inc(s["count_mm"], 1)
            pe.wait_ge(s["counted"], 32)
            pe.matmul(ps[:, 2, 0:1], same[:], cnt[:], start=True, stop=True).then_inc(s["count_mm"], 1)
            pe.wait_ge(s["ready"], 1)
            pe.matmul(ps[:, 3, 0:1], earlier[:], run[:, C - 1:C], start=True, stop=True).then_inc(s["pre_mm"], 1)
            pe.wait_ge(s["ready"], 2)
            pe.matmul(ps[:, 3, 0:1], earlier[:], run[:, C - 1:C], start=True, stop=True).then_inc(s["pre_mm"], 1)
            for b in range(B):
                mm = pe.matmul(ps[:, 4, b:b + 1], pick[:, b, :], na[:], start=True, stop=True)
            mm.then_inc(s["pre_mm"], 1)
            for j in range(C):
                pe.wait_ge(s["hot"], j + 1)
                pe.matmul(ps[0:2 * B, 5, :], vals[:, j, :], hot[:, j % 4, :], start=(j == 0),
                          stop=(j == C - 1)).then_inc(s["hot_mm"], 1)
            pe.wait_ge(s["found"], 1)
            for n in range(CC):
                mm = pe.transpose(ps[:, 6, n * 2 * B:(n + 1) * 2 * B], found[:, n * P:(n + 1) * P],
                                  c["ident"][0:2 * B, 0:2 * B])
            mm.then_inc(s["found_mm"], 1)

        @block.vector
        def _(dve):
            steps = [0]

            def link(op):
                steps[0] += 1
                op.then_inc(s["step"], 1)
                dve.wait_ge(s["step"], steps[0])

            dve.wait_ge(s["flat_mm"], 1)
            dve.tensor_copy(flat[:], ps[0:NT, 0, 0:P]).then_inc(s["flat"], 1)
            link(dve.memset(ones[:], 1.0))
            link(dve.memset(na[:], math.log(SEQ) - LOGK))
            link(dve.memset(edge[:].bitcast(F32), 0.0))
            link(dve.memset(bit[:].bitcast(F32), 2.0))
            dve.wait_ge(s["s_in"], 16)
            link(dve.tensor_reduce(top[:], sco[:], AX, ALU.max))
            link(dve.tensor_scalar(wide[:], ones[:, 0:R], top[:], None, ALU.mult))
            link(dve.transpose(wideT[:], wide[:]))
            link(dve.tensor_reduce(smax[:], wideT[:], AX, ALU.max))
            with dve.Fori(0, ITERS - 1) as i:
                dve.wait_ge(s["na"], i)
                dve.tensor_scalar(nm[:], na[:], smax[:], -1.0, ALU.min, ALU.mult)
                dve.tensor_scalar(sbv[:], sco[:], na[:], None, ALU.min).then_inc(s["shifted"], 1)
                dve.wait_ge(s["logged"], i + 1)
                dve.tensor_scalar(na[:], lse[:], nm[:], LOGK, ALU.subtract, ALU.subtract).then_inc(s["na"], 1)
            dve.wait_ge(s["na"], ITERS - 1)
            link(dve.tensor_scalar(u[:], sco[:], na[:], -1.0, ALU.subtract, ALU.mult))
            link(dve.tensor_scalar(u[:], u[:], 0.0, 104.0, ALU.max, ALU.min))
            with dve.Fori(0, 31) as i:
                dve.wait_ge(s["edge"], i)
                dve.tensor_tensor(cand[:], edge[:], bit[:], ALU.bitwise_or).then_inc(s["cand"], 1)
                dve.wait_ge(s["cand"], i + 1)
                dve.tensor_scalar(below[:], u[:], cand[:].bitcast(F32), 0.0, ALU.is_lt, ALU.add,
                                  accum_out=cnt[:]).then_inc(s["counted"], 1)
                dve.tensor_scalar(bit[:], bit[:], 1, None, ALU.logical_shift_right).then_inc(s["shift"], 1)
                dve.wait_ge(s["count_mm"], i + 1)
                dve.tensor_scalar(few[:], ps[:, 2, 0:1], float(ROUTED), None, ALU.is_lt).then_inc(s["shift"], 1)
                dve.wait_ge(s["shift"], 2 * i + 2)
                dve.tensor_scalar(wide[:, 0:1], ones[:, 0:1], 1.0, None, ALU.mult)
                dve.copy_predicated(edge[:], few[:], cand[:]).then_inc(s["edge"], 1)
            dve.wait_ge(s["edge"], 31)
            dve.tensor_scalar(below[:], u[:], edge[:].bitcast(F32), 0.0, ALU.is_lt, ALU.add,
                              accum_out=cnt[:]).then_inc(s["counted"], 1)
            link(dve.tensor_scalar(equal[:], u[:], edge[:].bitcast(F32), None, ALU.is_equal))
            dve.wait_ge(s["count_mm"], 32)
            link(dve.tensor_scalar(need[:], ps[:, 2, 0:1], -1.0, float(ROUTED), ALU.mult, ALU.add))
            dve.tensor_tensor_scan(run[:], ones[:], equal[:], 0.0, ALU.mult, ALU.add).then_inc(s["ready"], 1)
            dve.wait_ge(s["pre_mm"], 1)
            link(dve.tensor_copy(pre[:], ps[:, 3, 0:1]))
            link(dve.tensor_scalar(sel[:], run[:], pre[:], need[:], ALU.add, ALU.is_le))
            link(dve.tensor_tensor(sel[:], sel[:], equal[:], ALU.mult))
            link(dve.tensor_tensor(sel[:], sel[:], below[:], ALU.add))
            dve.tensor_tensor_scan(run[:], ones[:], sel[:], 0.0, ALU.mult, ALU.add).then_inc(s["ready"], 1)
            dve.wait_ge(s["pre_mm"], 2)
            link(dve.tensor_copy(pre[:], ps[:, 3, 0:1]))
            link(dve.tensor_scalar(pos[:], run[:], pre[:], None, ALU.add))
            link(dve.tensor_tensor(pos[:], pos[:], sel[:], ALU.mult))
            link(dve.tensor_scalar(pos[:], pos[:], -1.0, None, ALU.add))
            dve.wait_ge(s["made"], MADE)
            link(dve.tensor_scalar(vals[:, :, 0:B], batch[:].unsqueeze(1).to_broadcast([P, C, B]), row[:], None,
                                   ALU.mult))
            link(dve.tensor_tensor(vals[:, :, B:2 * B], batch[:].unsqueeze(1).to_broadcast([P, C, B]),
                                   col[:].unsqueeze(2).to_broadcast([P, C, B]), ALU.mult))
            for j in range(C):
                if j >= 4:
                    dve.wait_ge(s["hot_mm"], j - 3)
                dve.tensor_scalar(hot[:, j % 4, :], slots[:], pos[:, j:j + 1], None, ALU.is_equal).then_inc(s["hot"], 1)
            dve.wait_ge(s["pre_mm"], 3)
            dve.tensor_copy(c["na"][:], ps[:, 4, 0:B])
            dve.wait_ge(s["hot_mm"], C)
            dve.tensor_copy(found[:], ps[0:2 * B, 5, :]).then_inc(s["found"], 1)
            dve.wait_ge(s["found_mm"], 1)
            got = ps[:, 6, 0:CC * 2 * B].rearrange("p (n w) -> p w n", w=2 * B)
            link(dve.tensor_copy(rows_f[:], got[:, B:2 * B, :]))
            link(dve.scalar_tensor_tensor(rows_f[:], got[:, 0:B, :], float(C), rows_f[:], ALU.mult, ALU.add))
            dve.tensor_copy(c["heavy_rows"][:], rows_f[:])


def heavy_phase(nc, a, scr, c, out):
    with ExitStack() as ctx:
        def sb(name, shape, dt=F32):
            return ctx.enter_context(nc.sbuf_tensor(f"h_{name}", shape, dt))

        xh = [sb(f"xh{q}", [P, CC, XS]) for q in range(2)]
        xT = sb("xT", [P, DC, CAP])
        hT = sb("hT", [P, HC, CAP])
        y = [sb(f"y{q}", [P, CC, D]) for q in range(2)]
        val, ex, rest, one = (sb(n, [P, CC]) for n in ("val", "ex", "rest", "one"))
        ps = c["ps"]
        s = Sems(nc, ctx, "h", "gathered0 gathered1 scattered x_mm xT val ex rest one h_mm h d_mm yb y")
        block = ctx.enter_context(nc.Block())

        @block.gpsimd
        def _(pool):
            def gather(b):
                if b >= 2:
                    pool.wait_ge(s["x_mm"], DC * (b - 1))
                    pool.wait_ge(s["val"], b - 1)
                for n in range(CC):
                    pool.indirect_dma_start(
                        out=xh[b % 2][:, n, :], out_offset=None, in_=scr["xs"][:, :],
                        in_offset=bass.IndirectOffsetOnAxis(ap=c["heavy_rows"][:, b, n:n + 1], axis=0),
                    ).then_inc(s[f"gathered{b % 2}"], 16)

            gather(0)
            for b in range(B):
                if b + 1 < B:
                    gather(b + 1)
                for n in range(CC):
                    pool.wait_ge(s["y"], CC * b + n + 1)
                    pool.indirect_dma_start(
                        out=out[:, :], out_offset=bass.IndirectOffsetOnAxis(ap=c["heavy_rows"][:, b, n:n + 1], axis=0),
                        in_=y[b % 2][:, n, :], in_offset=None, compute_op=ALU.add).then_inc(s["scattered"], 16)
            pool.wait_ge(s["scattered"], 16 * CC * B)

        def turns(engine, body):
            with engine.Fori(0, B // 2) as j:
                body(2 * j, j, 0)
                body(2 * j + 1, j, 1)

        @block.vector
        def _(dve):
            dve.wait_ge(c["hw_in"], 80)

            def batch(b, j, q):
                dve.wait_ge(s[f"gathered{q}"], 16 * CC * (j + 1))
                dve.tensor_scalar(val[:], xh[q][:, :, D], c["na"][:, bass.ds(b, 1)], 0.0, ALU.subtract,
                                  ALU.min).then_inc(s["val"], 1)
                for k in range(DC):
                    dve.wait_ge(s["x_mm"], DC * b + k + 1)
                    dve.tensor_scalar(xT[:, k, :], ps[:, 4 + k % 2, :], c["hgam"][:, k:k + 1], None,
                                      ALU.mult).then_inc(s["xT"], 1)
                dve.wait_ge(s["ex"], b + 1)
                dve.tensor_scalar(rest[:], ex[:], -1.0, 1.0, ALU.mult, ALU.add).then_inc(s["rest"], 1)
                dve.wait_ge(s["rest"], b + 1)
                dve.tensor_tensor(one[:], ex[:], rest[:], ALU.add).then_inc(s["one"], 1)
                for n in range(CC):
                    dve.wait_ge(s["d_mm"], CC * b + n + 1)
                    if n == 0:
                        dve.wait_ge(s["scattered"], 16 * CC * b)
                    dve.tensor_tensor(y[q][:, n, :], ps[:, 6 + n % 2, :], c["hb2"][:], ALU.add).then_inc(s["yb"], 1)
                    dve.wait_ge(s["yb"], CC * b + n + 1)
                    dve.tensor_scalar(y[q][:, n, :], y[q][:, n, :], one[:, n:n + 1], None,
                                      ALU.mult).then_inc(s["y"], 1)

            turns(dve, batch)

        @block.scalar
        def _(act):
            act.wait_ge(c["hw_in"], 80)

            def batch(b, j, q):
                act.wait_ge(s["val"], b + 1)
                act.wait_ge(s["one"], b)
                act.activation(ex[:], val[:], ACT.Exp).then_inc(s["ex"], 1)
                for f in range(HC):
                    act.wait_ge(s["h_mm"], HC * b + f + 1)
                    act.activation(hT[:, f, :], ps[:, f % 4, :], ACT.Gelu, bias=c["hb1"][:, f:f + 1]).then_inc(s["h"], 1)

            turns(act, batch)

        @block.tensor
        def _(pe):
            pe.wait_ge(c["hw_in"], 80)

            def batch(b, j, q):
                pe.wait_ge(s[f"gathered{q}"], 16 * CC * (j + 1))
                for k in range(DC):
                    if k >= 2:
                        pe.wait_ge(s["xT"], DC * b + k - 1)
                    for n in range(CC):
                        mm = pe.transpose(ps[:, 4 + k % 2, n * P:(n + 1) * P], xh[q][:, n, k * P:(k + 1) * P],
                                          c["ident"][:])
                    mm.then_inc(s["x_mm"], 1)
                pe.wait_ge(s["xT"], DC * b + DC)
                for f in range(HC):
                    if f >= 4:
                        pe.wait_ge(s["h"], HC * b + f - 3)
                    for k in range(DC):
                        mm = pe.matmul(ps[:, f % 4, :], c["hw1"][:, k, f * P:(f + 1) * P], xT[:, k, :],
                                       start=(k == 0), stop=(k == DC - 1))
                    mm.then_inc(s["h_mm"], 1)
                pe.wait_ge(s["h"], HC * b + HC)
                for n in range(CC):
                    if n < 2:
                        pe.wait_ge(s["y"], CC * b)
                    else:
                        pe.wait_ge(s["yb"], CC * b + n - 1)
                    for f in range(HC):
                        mm = pe.matmul(ps[:, 6 + n % 2, :], hT[:, f, n * P:(n + 1) * P], c["hw2"][:, f, :],
                                       start=(f == 0), stop=(f == HC - 1))
                    mm.then_inc(s["d_mm"], 1)

            turns(pe, batch)


def build(nc, a, out):
    scr = {}
    for l in range(2):
        scr[f"kbd{l}"] = nc.dram_tensor(f"kbd{l}_dram", (B, P, GROUPS * HG * KEYS), F32).ap()
        scr[f"vm{l}"] = nc.dram_tensor(f"vm{l}_dram", (B, P, D), F32).ap()
        scr[f"vt{l}"] = nc.dram_tensor(f"vt{l}_dram", (B, TROWS, D), F32).ap()
    scr["delta"] = nc.dram_tensor("delta_dram", (B, P, KEYS), F32).ap()
    scr["x1"] = nc.dram_tensor("x1_dram", (NTOK + CAP, D), F32).ap()
    scr["xw"] = nc.dram_tensor("xw_dram", (NTOK + CAP, XW), F32).ap()
    scr["xs"] = nc.dram_tensor("xs_dram", (NTOK, XS), F32).ap()
    scr["scores"] = nc.dram_tensor("scores_dram", (NTOK,), F32).ap()
    with ExitStack() as ctx:
        c = {}
        constants(nc, ctx, c)
        key_value_phase(nc, a, scr, c)
        with ExitStack() as part:
            def keep(name, shape, dt=F32):
                c[name] = part.enter_context(nc.sbuf_tensor(f"c_{name}", shape, dt))

            keep("logits", [P, NT * E])
            keep("top8", [P, NT * TOPK])
            keep("expert_rows", [P, E * CC], I32)
            token_phase(nc, 0, a, scr, c, a["x"], scr["x1"])
            expert_slots_phase(nc, a, scr, c)
            expert_phase(nc, a, scr, c)
        with ExitStack() as part:
            def keep(name, shape, dt=F32):
                c[name] = part.enter_context(nc.sbuf_tensor(f"c_{name}", shape, dt))

            keep("scores", [P, NT])
            token_phase(nc, 1, a, scr, c, scr["x1"], out)
            keep("hw1", [P, DC, HEAVY])
            keep("hw2", [P, HC, D])
            keep("hb1", [P, HC])
            keep("hb2", [P, D])
            keep("hgam", [P, DC])
            keep("na", [P, B])
            keep("heavy_rows", [P, B, CC], I32)
            c["hw_in"] = part.enter_context(nc.semaphore("heavy_weights_in"))
            routing_phase(nc, a, scr, c)
            heavy_phase(nc, a, scr, c, out)


def kernel(**inputs):
    import numpy as np
    import concourse.bacc as bacc
    from concourse.bass_utils import run_bass_kernel_spmd

    def turned(v):
        return np.ascontiguousarray(np.swapaxes(np.asarray(v), -1, -2))

    host = {
        "x": np.asarray(inputs["x"]).reshape(NTOK, D),
        "ctxT": turned(inputs["ctx_1024"]),
        "tau": np.asarray(inputs["condB_tau"]),
        "delta": np.asarray(inputs["fside_BxS2_0"]),
        "gateT": turned(inputs["L0_ffn_gate_weight"]),
        "gate_upT": turned(inputs["L0_ffn_gate_up_proj"]).reshape(E * D, 2 * F),
        "downT": turned(inputs["L0_ffn_down_proj"]).reshape(E * F, D),
        "routing": np.asarray(inputs["L1_ffn_routing_token"]),
    }
    for l in range(2):
        for n in "qkvo":
            host[f"W{n}T{l}"] = turned(inputs[f"L{l}_xcond_W{n}"])
            host[f"b{n}{l}"] = np.asarray(inputs[f"L{l}_xcond_b{n}"])
    for n in ("light", "heavy"):
        for m in ("gamma", "w1", "b1", "w2", "b2"):
            host[f"{n}_{m}"] = np.asarray(inputs[f"L1_ffn_{n}_{m}"])

    nc = bacc.Bacc("TRN2", target_bir_lowering=False, num_devices=1)
    arrays, a = {}, {}
    for name, v in host.items():
        v = np.ascontiguousarray(v)
        arrays[f"in_{name}"] = v
        a[name] = nc.dram_tensor(f"in_{name}", v.shape, mybir.dt.from_np(v.dtype), kind="ExternalInput").ap()
    out = nc.dram_tensor("out_rows", (NTOK, D), F32, kind="ExternalOutput").ap()
    build(nc, a, out)
    r = run_bass_kernel_spmd(nc, [arrays], core_ids=[0])
    return r.results[0]["out_rows"].reshape(B, SEQ, D)
```

```python
from contextlib import ExitStack
import math

import concourse.bass as bass
from concourse import mybir

F32 = mybir.dt.float32
F32R = mybir.dt.float32r
BF16 = mybir.dt.bfloat16
I32 = mybir.dt.int32
ALU = mybir.AluOpType
ACT = mybir.ActivationFunctionType
AX = mybir.AxisListType.X

P = 128
B, SEQ, D = 4, 2048, 512
NTOK = B * SEQ
KEYS = 154
KTAIL = KEYS - P
HEADS, DK = 16, 32
HG = P // DK
GROUPS = HEADS // HG
TROWS = HG * KTAIL
DC = D // P
TG = 4
GTOK = TG * P
NG = NTOK // GTOK
NT = NTOK // P
E, F, CAP, TOPK = 32, 384, 512, 8
FC = F // P
CC = CAP // P
ROUTED = 512
ITERS = 50
EFF_K = min(ROUTED * 9.0 / 8.0, SEQ)
LIGHT, HEAVY = 256, 2048
HC = HEAVY // P
XW = D + E
XS = D + 4
EPS = 1e-5
UNITS = TG * GROUPS


class Sems:

    def __init__(self, nc, ctx, tag, names):
        self.by = {n: nc.alloc_semaphore(f"{tag}_{n}") for n in names.split()}

        def give_back():
            nc.clear_and_free_semaphores(list(self.by.values()))
            nc.all_engine_barrier()

        ctx.callback(give_back)

    def __getitem__(self, name):
        return self.by[name]


def high_of(engine, out, src):
    return engine.tensor_copy(out, src)


def product(pe, out, left, right, start, stop):
    pe.matmul(out, left[0], right[0], start=start, stop=False)
    pe.matmul(out, left[0], right[1], start=False, stop=False)
    return pe.matmul(out, left[1], right[0], start=False, stop=stop)


def rows(dram, group, width=None):
    v = dram[bass.ds(group * GTOK, GTOK), 0:width] if width else dram[bass.ds(group * GTOK, GTOK), :]
    return v.rearrange("(s p) d -> p s d", p=P)


def constants(nc, ctx, c):
    c["ident"] = ctx.enter_context(nc.sbuf_tensor("ident", [P, P], F32))
    c["ps"] = ctx.enter_context(nc.psum_tensor("ps", [P, 8, 512], F32))
    with ExitStack() as own:
        s = Sems(nc, own, "cst", "zero")
        block = own.enter_context(nc.Block())

        @block.gpsimd
        def _(pool):
            pool.memset(c["ident"][:], 0.0).then_inc(s["zero"], 1)
            pool.wait_ge(s["zero"], 1)
            pool.affine_select(out=c["ident"][:], in_=c["ident"][:], compare_op=ALU.not_equal, fill=1.0,
                               base=0, pattern=[[-1, P]], channel_multiplier=1)


def key_value_phase(nc, a, scr, c):
    with ExitStack() as ctx:
        def sb(name, shape, dt=F32):
            return ctx.enter_context(nc.sbuf_tensor(f"kv_{name}", shape, dt))

        ctxT = sb("ctxT", [P, DC, B, KEYS])
        wk, wv = sb("wk", [P, DC, D]), sb("wv", [P, DC, D])
        bk, bv = sb("bk", [P, DC]), sb("bv", [P, D])
        tau = sb("tau", [P, B])
        delta = sb("delta", [P, B, KEYS])
        kbd = sb("kbd", [P, B, GROUPS, HG * KEYS])
        vm, vt = sb("vm", [P, B, D]), sb("vt", [KTAIL, B, D])
        zero = sb("zero", [TROWS, D])
        ps = c["ps"]
        s = Sems(nc, ctx, "kv", "zeroed ctx_in w_in scaled matmul evacuated cleared stored")
        JOBS = 16
        block = ctx.enter_context(nc.Block())

        @block.sync
        def _(sp):
            for b in range(B):
                sp.dma_start(ctxT[:, :, b, :],
                             a["ctxT"][b].rearrange("(k p) n -> p k n", p=P)).then_inc(s["ctx_in"], 16)
            sp.dma_start(tau[:], a["tau"].partition_broadcast(P)).then_inc(s["ctx_in"], 16)
            sp.dma_start(delta[:], a["delta"].rearrange("b n -> (b n)").partition_broadcast(P)
                         .rearrange("p (b n) -> p b n", b=B)).then_inc(s["ctx_in"], 16)
            sp.wait_ge(s["zeroed"], 2)
            for l in range(2):
                for b in range(B):
                    sp.dma_start(scr[f"vt{l}"][b], zero[:]).then_inc(s["cleared"], 16)
            sp.wait_ge(s["cleared"], 16 * 2 * B)
            for l in range(2):
                sp.wait_ge(s["evacuated"], JOBS * l)
                sp.dma_start(wk[:], a[f"WkT{l}"].rearrange("(k p) n -> p k n", p=P)).then_inc(s["w_in"], 16)
                sp.dma_start(wv[:], a[f"WvT{l}"].rearrange("(k p) n -> p k n", p=P)).then_inc(s["w_in"], 16)
                sp.dma_start(bv[:], a[f"bv{l}"].partition_broadcast(P)).then_inc(s["w_in"], 16)
                with nc.allow_non_contiguous_dma(reason="a bias by partition"):
                    sp.dma_start(bk[:], a[f"bk{l}"].rearrange("(k p) -> p k", p=P)).then_inc(s["w_in"], 16)
                sp.wait_ge(s["evacuated"], JOBS * (l + 1))
                for b in range(B):
                    sp.dma_start(scr[f"kbd{l}"][b], kbd[:, b]).then_inc(s["stored"], 16)
                    sp.dma_start(scr[f"vm{l}"][b], vm[:, b]).then_inc(s["stored"], 16)
                    for h in range(HG):
                        sp.dma_start(
                            scr[f"vt{l}"][b].rearrange("(n h) (g e d) -> n h g e d", h=HG, e=HG, d=DK)[:, h, :, h, :],
                            vt[:, b].rearrange("n (g e d) -> n g e d", e=HG, d=DK)[:, :, h, :],
                        ).then_inc(s["stored"], 16)
            sp.wait_ge(s["scaled"], 2)
            for b in range(B):
                sp.dma_start(scr["delta"][b], delta[:, b]).then_inc(s["stored"], 16)
            sp.wait_ge(s["stored"], 16 * (2 * (2 + HG) * B + B))

        @block.tensor
        def _(pe):
            pe.wait_ge(s["ctx_in"], 16 * (B + 2))
            for l in range(2):
                pe.wait_ge(s["w_in"], 64 * (l + 1))
                for j in range(JOBS):
                    bank = j % 8
                    if JOBS * l + j >= 8:
                        pe.wait_ge(s["evacuated"], JOBS * l + j - 7)
                    if j < 8:
                        n, half = j // 2, j % 2
                        for k in range(DC):
                            mm = pe.matmul(ps[:, bank, 0:2 * KEYS], wk[:, k, n * P:(n + 1) * P],
                                           ctxT[:, k, 2 * half:2 * half + 2, 0:KEYS],
                                           start=(k == 0), stop=(k == DC - 1))
                    elif j < 12:
                        for k in range(DC):
                            mm = pe.matmul(ps[:, bank, :], ctxT[:, k, j - 8, 0:P], wv[:, k, :],
                                           start=(k == 0), stop=(k == DC - 1))
                    else:
                        for k in range(DC):
                            mm = pe.matmul(ps[0:KTAIL, bank, :], ctxT[:, k, j - 12, P:KEYS], wv[:, k, :],
                                           start=(k == 0), stop=(k == DC - 1))
                    mm.then_inc(s["matmul"], 1)

        @block.vector
        def _(dve):
            dve.memset(kbd[:], 0.0).then_inc(s["zeroed"], 1)
            dve.memset(zero[:], 0.0).then_inc(s["zeroed"], 1)
            dve.wait_ge(s["zeroed"], 2)
            dve.wait_ge(s["ctx_in"], 16 * (B + 2))
            dve.tensor_scalar(tau[:], tau[:], 1.0 / math.sqrt(DK), None, ALU.mult).then_inc(s["scaled"], 1)
            dve.tensor_scalar(delta[:], delta[:], 1.0 / math.sqrt(DK), None, ALU.mult).then_inc(s["scaled"], 1)
            dve.wait_ge(s["scaled"], 2)
            for l in range(2):
                dve.wait_ge(s["w_in"], 64 * (l + 1))
                if l:
                    dve.wait_ge(s["stored"], 16 * (2 + HG) * B)
                for j in range(JOBS):
                    bank = j % 8
                    dve.wait_ge(s["matmul"], JOBS * l + j + 1)
                    if j < 8:
                        n, half = j // 2, j % 2
                        for b in (2 * half, 2 * half + 1):
                            for g in range(HG):
                                r = slice(DK * g, DK * (g + 1))
                                op = dve.tensor_scalar(kbd[r, b, n, g * KEYS:(g + 1) * KEYS],
                                                       ps[r, bank, (b % 2) * KEYS:(b % 2 + 1) * KEYS],
                                                       bk[r, n:n + 1], tau[r, b:b + 1], ALU.add, ALU.mult)
                    elif j < 12:
                        op = dve.tensor_tensor(vm[:, j - 8, :], ps[:, bank, :], bv[:], ALU.add)
                    else:
                        op = dve.tensor_tensor(vt[:, j - 12, :], ps[0:KTAIL, bank, :], bv[0:KTAIL, :], ALU.add)
                    op.then_inc(s["evacuated"], 1)


def reached(engine, sem, value):
    if not (isinstance(value, int) and value <= 0):
        engine.wait_ge(sem, value)


def token_phase(nc, l, a, scr, c, x_in, x_rows):
    gate = l == 0
    with ExitStack() as ctx:
        def sb(name, shape, dt=F32):
            return ctx.enter_context(nc.sbuf_tensor(f"t{l}_{name}", shape, dt))

        wq, wo = sb("wq", [P, DC, D]), sb("wo", [P, DC, D])
        bq, bo = sb("bq", [P, DC]), sb("bo", [P, D])
        kbd = sb("kbd", [P, GROUPS, HG * KEYS])
        vm, vt = sb("vm", [P, D]), sb("vt", [TROWS, D])
        deltas, delta = sb("deltas", [P, B, KEYS]), sb("delta", [P, KEYS])
        x, xhold, xbo = sb("x", [P, TG, D]), sb("xhold", [P, TG, D]), sb("xbo", [P, TG, D])
        xn, xnT, qT, oT = (sb(n, [P, TG, D]) for n in ("xn", "xnT", "qT", "oT"))
        xs = sb("xs", [P, TG, D])
        sc = sb("sc", [P, 2, HG, KEYS])
        pr = sb("pr", [P, 4, KEYS, HG])
        pTm, pTt = sb("pTm", [P, 2, HG, D]), sb("pTt", [TROWS, D])
        negmax, total, inv = (sb(n, [P, UNITS, HG]) for n in ("negmax", "total", "inv"))
        stat, mv = sb("stat", [P, 2, TG, 6]), sb("mv", [P, 2, TG, 2])
        ve, rstd = sb("ve", [P, 2, TG]), sb("rstd", [P, 2, TG])
        half, eps, tick = (sb(n, [P, TG]) for n in ("half", "eps", "tick"))
        zero = sb("zero", [P, D])
        z = sb("z", [P, TG, D if gate else XS])
        zT = sb("zT", [P, TG, D])
        if gate:
            wg = sb("wg", [P, DC, E])
            part = sb("part", [P, GTOK])
            logit, top = sb("logit", [P, TG, E]), sb("top", [P, TG, TOPK])
        else:
            w1, w2 = sb("w1", [P, DC, LIGHT]), sb("w2", [P, LIGHT // P, D])
            gam, b1, b2 = sb("gam", [P, DC]), sb("b1", [P, LIGHT // P]), sb("b2", [P, D])
            rt = sb("rt", [P, D])
            hT = sb("hT", [P, LIGHT // P, D])
            junk, junk2 = sb("junk", [P, D]), sb("junk2", [P, D])
            ssq, rn, score = sb("ssq", [P, TG]), sb("rn", [P, TG]), sb("score", [P, TG])
        ps = c["ps"]
        s = Sems(nc, ctx, f"t{l}",
                 "w_in kv_in0 kv_in1 kv_in2 kv_in3 x_in ready x_stored z_stored y_stored "
                 "x_stats x_mv x_ve x_rstd xn xheld xbo xnT_mm xnT_dve xnT_act q_mm q_out delta "
                 "scored added negmax exped inv normed p_mm pTm pTt pv oT_out proj resid "
                 "s_stats s_mv s_ve s_rstd xl z z_mm zT_dve zT_act side_mm side_out top "
                 "ssq ssq_c rn score xb2 h_mm h_out part_mm part logit")
        block = ctx.enter_context(nc.Block())
        W_IN = (16 * 6 if gate else 16 * 11)
        Q_BANK = (6, 7, 7, 6 if gate else 5)

        def turns(engine, body):
            body(-1, False, False, True, True)
            body(0, False, True, True, True)
            body(1, True, True, True, True)
            with engine.Fori(2, NG - 2) as i:
                body(i, True, True, True, True)
            body(NG - 2, True, True, True, False)
            body(NG - 1, True, True, False, False)
            body(NG, True, False, False, False)

        def load_kv(sp, j, g, used=0):
            b = j // (NG // B)
            n = HG * KEYS
            loads = []
            for dst, src, r, cols in ((kbd[:, g, :], "kbd%d" % l, P, slice(g * n, (g + 1) * n)),
                                      (vm[:, g * P:(g + 1) * P], "vm%d" % l, P, slice(g * P, (g + 1) * P)),
                                      (vt[:, g * P:(g + 1) * P], "vt%d" % l, TROWS, slice(g * P, (g + 1) * P))):
                loads.append((dst, scr[src].rearrange("b p n -> (b p) n")[bass.ds(b * r, r), cols]))
            reached(sp, s["pv"], used)
            for dst, v in loads:
                sp.dma_start(dst, v).then_inc(s[f"kv_in{g}"], 16)

        @block.sync
        def _(sp):
            sp.dma_start(x[:], rows(x_in, 0)).then_inc(s["x_in"], 16)
            sp.dma_start(wq[:], a[f"WqT{l}"].rearrange("(k p) n -> p k n", p=P)).then_inc(s["w_in"], 16)
            with nc.allow_non_contiguous_dma(reason="biases by partition"):
                sp.dma_start(bq[:], a[f"bq{l}"].rearrange("(k p) -> p k", p=P)).then_inc(s["w_in"], 16)
                if not gate:
                    sp.dma_start(gam[:], a["light_gamma"].rearrange("(k p) -> p k", p=P)).then_inc(s["w_in"], 16)
                    sp.dma_start(b1[:], a["light_b1"].rearrange("(k p) -> p k", p=P)).then_inc(s["w_in"], 16)
            sp.dma_start(bo[:], a[f"bo{l}"].partition_broadcast(P)).then_inc(s["w_in"], 16)
            sp.dma_start(deltas[:], scr["delta"].rearrange("b p n -> p b n")).then_inc(s["w_in"], 16)
            for g in range(GROUPS):
                load_kv(sp, 0, g)
            sp.dma_start(wo[:], a[f"WoT{l}"].rearrange("(k p) n -> p k n", p=P)).then_inc(s["w_in"], 16)
            if gate:
                sp.dma_start(wg[:], a["gateT"].rearrange("(k p) n -> p k n", p=P)).then_inc(s["w_in"], 16)
            else:
                sp.dma_start(rt[:], a["routing"].partition_broadcast(P)).then_inc(s["w_in"], 16)
                sp.dma_start(b2[:], a["light_b2"].partition_broadcast(P)).then_inc(s["w_in"], 16)
                sp.dma_start(w1[:], a["light_w1"].rearrange("(k p) n -> p k n", p=P)).then_inc(s["w_in"], 16)
                sp.dma_start(w2[:], a["light_w2"].rearrange("(k p) n -> p k n", p=P)).then_inc(s["w_in"], 16)

            def turn(i, prev, cur, nxt, nxt2):
                if prev and cur:
                    load_kv(sp, i, GROUPS - 1, GROUPS * i)
                if prev and gate:
                    sp.wait_ge(s["resid"], TG * i)
                    sp.dma_start(rows(x_rows, i - 1), xs[:]).then_inc(s["x_stored"], 16)
                if cur and nxt:
                    load_kv(sp, i + 1, 0, GROUPS * i + 1)
                if nxt2:
                    reached(sp, s["xheld"], TG * (i + 2))
                    reached(sp, s["xn"], TG * (i + 2))
                    sp.dma_start(x[:], rows(x_in, i + 2)).then_inc(s["x_in"], 16)
                if prev:
                    sp.wait_ge(s["z"], TG * i)
                    if gate:
                        sp.dma_start(rows(scr["xw"], i - 1, D), z[:]).then_inc(s["z_stored"], 16)
                    else:
                        sp.wait_ge(s["score"], i)
                        sp.dma_start(rows(scr["xs"], i - 1), z[:]).then_inc(s["z_stored"], 16)
                if cur and nxt:
                    for g in (1, 2):
                        load_kv(sp, i + 1, g, GROUPS * i + g + 1)
                if prev and not gate:
                    sp.wait_ge(s["side_out"], TG * i)
                    sp.dma_start(rows(x_rows, i - 1), xs[:]).then_inc(s["y_stored"], 16)

            turns(sp, turn)
            sp.wait_ge(s["z_stored"], 16 * NG)
            sp.wait_ge(s["x_stored" if gate else "y_stored"], 16 * NG)

        @block.gpsimd
        def _(pool):
            pool.memset(half[:], -0.5).then_inc(s["ready"], 1)
            pool.memset(eps[:], EPS).then_inc(s["ready"], 1)
            pool.memset(zero[:], 0.0).then_inc(s["ready"], 1)
            if not gate:
                pool.memset(z[:, :, D:XS], 0.0).then_inc(s["ready"], 1)
            pool.wait_ge(s["ready"], 3 if gate else 4)

            def rstd_of(which, kind, n):
                pool.wait_ge(s[kind + "_mv"], TG * n + TG)
                pool.tensor_tensor(ve[:, which, :], mv[:, which, :, 1], eps[:], ALU.add).then_inc(s[kind + "_ve"], 1)
                pool.wait_ge(s[kind + "_ve"], n + 1)
                pool.tensor_tensor(rstd[:, which, :], ve[:, which, :], half[:],
                                   ALU.pow).then_inc(s[kind + "_rstd"], 1)

            rstd_of(0, "x", 0)
            pool.wait_ge(s["w_in"], W_IN)

            def normalize(i, v):
                reached(pool, s["inv"], UNITS * i + v + 1)
                p = pr[:, v % 4]
                pool.tensor_tensor(p, p, inv[:, v, :].unsqueeze(1).to_broadcast([P, KEYS, HG]),
                                   ALU.mult).then_inc(s["normed"], 1)

            def turn(i, prev, cur, nxt, nxt2):
                for st in range(UNITS):
                    if st >= 1 and cur:
                        normalize(i, st - 1)
                    if st == 0 and prev:
                        normalize(i - 1, UNITS - 1)
                    if st == 7 and prev:
                        rstd_of(1, "s", i - 1)
                    for t in {4: (0,), 5: (1, 2), 7: (3,)}.get(st, ()):
                        if cur:
                            reached(pool, s["resid"], TG * (i - 1) + t + 1)
                            reached(pool, s["xheld"], TG * i + t + 1)
                            pool.tensor_tensor(xbo[:, t, :], xhold[:, t, :], bo[:], ALU.add).then_inc(s["xbo"], 1)
                        if nxt:
                            reached(pool, s["xbo"], TG * i + t + 1)
                            reached(pool, s["x_in"], 16 * (i + 2))
                            pool.tensor_tensor(xhold[:, t, :], x[:, t, :], zero[:], ALU.add).then_inc(s["xheld"], 1)
                    if st == 9 and prev and not gate:
                        pool.wait_ge(s["ssq_c"], i)
                        pool.tensor_tensor(rn[:], ssq[:], half[:], ALU.pow).then_inc(s["rn"], 1)
                    if 10 <= st < 10 + TG and prev and not gate:
                        pool.wait_ge(s["xl"], TG * i)
                        pool.tensor_tensor(xs[:, st - 10, :], xs[:, st - 10, :], b2[:], ALU.add).then_inc(s["xb2"], 1)
                    if st == 12 and nxt2:
                        rstd_of(0, "x", i + 2)

            turns(pool, turn)

        @block.vector
        def _(dve):
            def statistics(which, kind, n, src, tiles):
                for t in tiles:
                    dve.bn_stats(stat[:, which, t, :], src[:, t, :]).then_inc(s[kind + "_stats"], 1)
                if TG - 1 not in tiles:
                    return
                dve.wait_ge(s[kind + "_stats"], TG * n + TG)
                dve.memset(tick[:], 0.0)
                for t in range(TG):
                    dve.bn_aggr(mv[:, which, t, :], stat[:, which, t, :]).then_inc(s[kind + "_mv"], 1)

            def normed(which, kind, n, src, dst, done, tiles=range(TG)):
                dve.wait_ge(s[kind + "_rstd"], n + 1)
                for t in tiles:
                    dve.tensor_scalar(dst[:, t, 0:D], src[:, t, :], mv[:, which, t, 0:1],
                                      rstd[:, which, t:t + 1], ALU.subtract, ALU.mult).then_inc(s[done], 1)

            dve.wait_ge(s["x_in"], 16)
            statistics(0, "x", 0, x, range(TG))
            normed(0, "x", 0, x, xn, "xn")
            dve.wait_ge(s["w_in"], W_IN)

            def add_and_max(i, u):
                dve.wait_ge(s["scored"], UNITS * i + u + 1)
                if u == 0:
                    dve.tensor_copy(delta[:], deltas[:, bass.ds(i // (NG // B), 1), :]).then_inc(s["delta"], 1)
                    dve.wait_ge(s["delta"], i + 1)
                reached(dve, s["exped"], UNITS * i + u - 1)
                dve.tensor_tensor(sc[:, u % 2].rearrange("p (b h) n -> p b h n", b=2),
                                  ps[:, 0:2, 0:2 * KEYS].rearrange("p b (h n) -> p b h n", h=2),
                                  delta[:].unsqueeze(1).unsqueeze(1).to_broadcast([P, 2, 2, KEYS]),
                                  ALU.add).then_inc(s["added"], 1)
                dve.wait_ge(s["added"], UNITS * i + u + 1)
                dve.tensor_reduce(negmax[:, u, :], sc[:, u % 2], AX, ALU.max,
                                  negate=True).then_inc(s["negmax"], 1)

            def inverse(i, v):
                dve.wait_ge(s["exped"], UNITS * i + v + 1)
                dve.reciprocal(inv[:, v, :], total[:, v, :]).then_inc(s["inv"], 1)

            def p_out(i, v):
                g, t = v // TG, v % TG
                dve.wait_ge(s["p_mm"], UNITS * i + v + 1)
                if t == 0:
                    reached(dve, s["pv"], GROUPS * i + g - 1)
                dve.tensor_copy(pTm[:, g % 2, :, t * P:(t + 1) * P],
                                ps[:, 2, :].rearrange("p (h n) -> p h n", h=HG)).then_inc(s["pTm"], 1)

            def residual(i, t):
                dve.wait_ge(s["proj"], TG * i + t + 1)
                if t == 0:
                    dve.wait_ge(s["xbo"], TG * (i + 1))
                    reached(dve, s["x_stored" if gate else "y_stored"], 16 * i)
                dve.tensor_tensor(xs[:, t, :], ps[:, 5 + t % 3, :], xbo[:, t, :], ALU.add).then_inc(s["resid"], 1)

            def transposed(i, k):
                dve.wait_ge(s["z_mm"], DC * i + k + 1)
                if k == 0:
                    reached(dve, s["part_mm"] if gate else s["h_mm"], i if gate else (LIGHT // P) * i)
                if gate:
                    dve.tensor_copy(zT[:, k, :], ps[:, 5, :]).then_inc(s["zT_dve"], 1)
                else:
                    dve.tensor_scalar(zT[:, k, :], ps[:, 5, :], gam[:, k:k + 1], None,
                                      ALU.mult).then_inc(s["zT_dve"], 1)

            def turn(i, prev, cur, nxt, nxt2):
                for st in range(UNITS):
                    if cur:
                        add_and_max(i, st)
                    if st == 0 and prev:
                        inverse(i - 1, UNITS - 1)
                    if st >= 1 and cur:
                        inverse(i, st - 1)
                    if st in (1, 2) and nxt:
                        k = 2 * (st - 1)
                        dve.wait_ge(s["xnT_mm"], DC * (i + 1) + k + 1)
                        reached(dve, s["q_mm"], DC * (i + 1))
                        dve.tensor_copy(xnT[:, k, :], ps[:, 6, :]).then_inc(s["xnT_dve"], 1)
                    if prev:
                        j = i - 1
                        if st == 3:
                            residual(j, 0)
                        if st == 4:
                            residual(j, 1)
                            residual(j, 2)
                        if st == 5:
                            residual(j, 3)
                        if st in (11, 12):
                            transposed(j, 2 * (st - 11))
                    if st < 2 and prev:
                        p_out(i - 1, UNITS - 2 + st)
                    if st >= 2 and cur:
                        p_out(i, st - 2)
                    if prev:
                        if st in (4, 5, 6):
                            tiles = {4: (0,), 5: (1, 2), 6: (3,)}[st]
                            dve.wait_ge(s["resid"], TG * j + tiles[-1] + 1)
                            statistics(1, "s", j, xs, tiles)
                        if st == 7:
                            reached(dve, s["z_stored"], 16 * j)
                            reached(dve, s["z_mm"], DC * j)
                            normed(1, "s", j, xs, z, "z" if gate else "xl")
                        if st == 8 and not gate:
                            dve.wait_ge(s["xl"], TG * i)
                            for t in range(TG):
                                dve.tensor_tensor_reduce(out=junk[:], in0=z[:, t, 0:D], in1=rt[:], scale=1.0,
                                                         scalar=0.0, op0=ALU.mult, op1=ALU.add,
                                                         accum_out=score[:, t:t + 1]).then_inc(s["top"], 1)
                                dve.wait_ge(s["top"], TG * j + t + 1)
                        if st == 9 and not gate:
                            dve.wait_ge(s["ssq"], TG * i)
                            dve.tensor_scalar(ssq[:], ssq[:], 1e-24, None, ALU.max).then_inc(s["ssq_c"], 1)
                        if st == 10 and not gate:
                            dve.wait_ge(s["rn"], i)
                            for t in range(TG):
                                dve.tensor_scalar(z[:, t, 0:D], z[:, t, 0:D], rn[:, t:t + 1], math.sqrt(D),
                                                  ALU.mult, ALU.mult).then_inc(s["z"], 1)
                            dve.tensor_copy(z[:, :, D], score[:]).then_inc(s["score"], 1)
                            dve.tensor_copy(c["scores"][:, bass.ds(j * TG, TG)], score[:])
                        if st == 14 and gate:
                            dve.wait_ge(s["side_mm"], i)
                            reached(dve, s["side_out"], j)
                            dve.tensor_reduce(logit[:], ps[:, 5, :].rearrange("p (t k e) -> p t e k", k=DC, e=E),
                                              AX, ALU.add).then_inc(s["logit"], 1)
                            dve.wait_ge(s["logit"], i)
                            dve.memset(tick[:], 0.0)
                            for t in range(TG):
                                op = dve.max(top[:, t, :], logit[:, t, :])
                            op.then_inc(s["top"], 1)
                            dve.tensor_copy(c["logits"][:, bass.ds(j * TG * E, TG * E)],
                                            logit[:].rearrange("p t e -> p (t e)"))
                            dve.wait_ge(s["top"], i)
                            dve.tensor_copy(c["top8"][:, bass.ds(j * TG * TOPK, TG * TOPK)],
                                            top[:].rearrange("p t k -> p (t k)")).then_inc(s["side_out"], 1)
                        if st == 15 and not gate:
                            dve.wait_ge(s["xb2"], TG * i)
                            for t in range(TG):
                                dve.wait_ge(s["side_mm"], TG * j + t + 1)
                                dve.tensor_tensor(xs[:, t, :], ps[:, 5 + (t + 2) % 3, :], xs[:, t, :],
                                                  ALU.add).then_inc(s["side_out"], 1)
                    if nxt2:
                        j = i + 2
                        if st == 10:
                            reached(dve, s["x_in"], 16 * (j + 1))
                            statistics(0, "x", j, x, (0, 1, 2))
                        if st == 11:
                            statistics(0, "x", j, x, (3,))
                        if st in (13, 14):
                            reached(dve, s["xnT_mm"], DC * j)
                            normed(0, "x", j, x, xn, "xn", (0, 1) if st == 13 else (2, 3))

            turns(dve, turn)

        @block.scalar
        def _(act):
            act.wait_ge(s["w_in"], W_IN)

            def query_out(j, n):
                act.wait_ge(s["q_mm"], DC * j + n + 1)
                reached(act, s["scored"], UNITS * (j - 1) + TG * (n + 1))
                act.activation(qT[:, n, :], ps[:, Q_BANK[n], :], ACT.Identity,
                               bias=bq[:, n:n + 1]).then_inc(s["q_out"], 1)

            def o_out(i, g):
                act.wait_ge(s["pv"], GROUPS * i + g + 1)
                reached(act, s["proj"], TG * i)
                act.copy(oT[:, g, :], ps[:, 4, :]).then_inc(s["oT_out"], 1)

            def p_tail_out(i, g):
                act.wait_ge(s["p_mm"], UNITS * i + TG * (g + 1))
                reached(act, s["pv"], GROUPS * i + g)
                act.copy(pTt[:], ps[0:TROWS, 3, :]).then_inc(s["pTt"], 1)

            def turn(i, prev, cur, nxt, nxt2):
                j = i - 1
                for st in range(UNITS):
                    if st == 3 and prev:
                        o_out(i - 1, GROUPS - 1)
                    if st in (7, 11, 15) and cur:
                        o_out(i, st // TG - 1)
                    if st in (1, 2) and nxt:
                        k = 2 * st - 1
                        act.wait_ge(s["xnT_mm"], DC * (i + 1) + k + 1)
                        reached(act, s["q_mm"], DC * (i + 1))
                        act.copy(xnT[:, k, :], ps[:, 7, :]).then_inc(s["xnT_act"], 1)
                    if st in (11, 12) and prev:
                        k = 2 * (st - 11) + 1
                        act.wait_ge(s["z_mm"], DC * j + k + 1)
                        if k == 1:
                            reached(act, s["part_mm"] if gate else s["h_mm"], j if gate else (LIGHT // P) * j)
                        if gate:
                            act.copy(zT[:, k, :], ps[:, 6, :]).then_inc(s["zT_act"], 1)
                        else:
                            act.activation(zT[:, k, :], ps[:, 6, :], ACT.Copy,
                                           scale=gam[:, k:k + 1]).then_inc(s["zT_act"], 1)
                    if cur:
                        u = st
                        act.wait_ge(s["negmax"], UNITS * i + u + 1)
                        reached(act, s["p_mm"], UNITS * i + u - 3)
                        for h in range(HG):
                            op = act.activation(pr[:, u % 4, :, h], sc[:, u % 2, h, :], ACT.Exp,
                                                bias=negmax[:, u, h:h + 1], accum_out=total[:, u, h:h + 1])
                        op.then_inc(s["exped"], 1)
                    if st == 0 and cur:
                        query_out(i, DC - 1)
                    if st in (7, 8, 12) and nxt:
                        query_out(i + 1, (7, 8, 12).index(st))
                    if st == 1 and prev:
                        p_tail_out(i - 1, GROUPS - 1)
                    if st in (5, 9, 13) and cur:
                        p_tail_out(i, st // TG - 1)
                    if prev:
                        if st == 8 and not gate:
                            reached(act, s["rn"], j)
                            for t in range(TG):
                                act.wait_ge(s["xl"], TG * j + t + 1)
                                act.activation(junk2[:], z[:, t, 0:D], ACT.Square,
                                               accum_out=ssq[:, t:t + 1]).then_inc(s["ssq"], 1)
                                act.wait_ge(s["ssq"], TG * j + t + 1)
                        if st == 13 and gate:
                            act.wait_ge(s["part_mm"], i)
                            reached(act, s["side_mm"], j)
                            act.copy(part[:], ps[:, 5, :]).then_inc(s["part"], 1)
                        if st == 14 and not gate:
                            for f in range(LIGHT // P):
                                act.wait_ge(s["h_mm"], (LIGHT // P) * j + f + 1)
                                if f == 0:
                                    reached(act, s["side_mm"], TG * j)
                                act.activation(hT[:, f, :], ps[:, 5 + f, :], ACT.Gelu,
                                               bias=b1[:, f:f + 1]).then_inc(s["h_out"], 1)

            turns(act, turn)

        @block.tensor
        def _(pe):
            ident = c["ident"]
            pe.wait_ge(s["w_in"], W_IN)

            def transposes(src, k, bank, done):
                for t in range(TG):
                    mm = pe.transpose(ps[:, bank, t * P:(t + 1) * P], src[:, t, k * P:(k + 1) * P], ident[:])
                mm.then_inc(done, 1)

            def scores(i, u):
                g, t = u // TG, u % TG
                if t == 0:
                    pe.wait_ge(s[f"kv_in{g}"], 48 * i + 48)
                    pe.wait_ge(s["q_out"], DC * i + g + 1)
                reached(pe, s["added"], UNITS * i + u)
                for hh in range(2):
                    mm = pe.matmul(ps[:, hh, 0:2 * KEYS], qT[:, g, t * P:(t + 1) * P],
                                   kbd[:, g, hh * 2 * KEYS:(hh + 1) * 2 * KEYS], start=True, stop=True)
                mm.then_inc(s["scored"], 1)

            def p_transposes(i, v):
                g, t = v // TG, v % TG
                pe.wait_ge(s["normed"], UNITS * i + v + 1)
                reached(pe, s["pTm"], UNITS * i + v)
                if t == 0:
                    reached(pe, s["pTt"], GROUPS * i + g)
                for h in range(HG):
                    pe.transpose(ps[:, 2, h * P:(h + 1) * P], pr[:, v % 4, 0:P, h], ident[:])
                pe.transpose(ps[0:TROWS, 3, t * P:(t + 1) * P], pr[:, v % 4, P:KEYS, :].rearrange("p n h -> p (n h)"),
                             ident[:]).then_inc(s["p_mm"], 1)

            def values(i, g):
                pe.wait_ge(s["pTm"], UNITS * i + TG * (g + 1))
                pe.wait_ge(s["pTt"], GROUPS * i + g + 1)
                reached(pe, s["oT_out"], GROUPS * i + g)
                pe.matmul(ps[:, 4, :], vt[:, g * P:(g + 1) * P], pTt[:], start=True, stop=False,
                          skip_group_check=True)
                for h in range(HG):
                    mm = pe.matmul(ps[h * DK:(h + 1) * DK, 4, :], vm[:, g * P + h * DK:g * P + (h + 1) * DK],
                                   pTm[:, g % 2, h, :], start=False, stop=True, skip_group_check=True)
                mm.then_inc(s["pv"], 1)

            def query(j, n, chunks):
                if 0 not in chunks:
                    pass
                elif n == 0:
                    pe.wait_ge(s["xnT_dve"], 2 * j + 2)
                    pe.wait_ge(s["xnT_act"], 2 * j + 2)
                    reached(pe, s["resid"], TG * (j - 2) + 2)
                elif n == 1:
                    reached(pe, s["resid"], TG * (j - 2) + 3)
                elif n == 2:
                    pe.wait_ge(s["q_out"], DC * j + 2)
                elif gate:
                    reached(pe, s["zT_act"], 2 * (j - 1))
                else:
                    reached(pe, s["side_out"], TG * (j - 2) + 2)
                for k in chunks:
                    mm = pe.matmul(ps[:, Q_BANK[n], :], wq[:, k, n * P:(n + 1) * P], xnT[:, k, :],
                                   start=(k == 0), stop=(k == DC - 1))
                if DC - 1 in chunks:
                    mm.then_inc(s["q_mm"], 1)

            def upto(n):
                return min(n, NG) if isinstance(n, int) else n

            def project(j, t):
                if t == 0:
                    pe.wait_ge(s["oT_out"], GROUPS * j + GROUPS)
                    if gate:
                        reached(pe, s["side_out"], j)
                    else:
                        pe.wait_ge(s["q_out"], DC * upto(j + 2))
                elif t == 1:
                    pe.wait_ge(s["xnT_dve"], 2 * upto(j + 3))
                elif t == 2:
                    pe.wait_ge(s["xnT_act"], 2 * upto(j + 3))
                else:
                    pe.wait_ge(s["resid"], TG * j + 1)
                for k in range(DC):
                    mm = pe.matmul(ps[:, 5 + t % 3, :], oT[:, k, t * P:(t + 1) * P], wo[:, k, :],
                                   start=(k == 0), stop=(k == DC - 1))
                mm.then_inc(s["proj"], 1)

            def hidden(j, f):
                for k in range(DC):
                    mm = pe.matmul(ps[:, 5 + f, :], w1[:, k, f * P:(f + 1) * P], zT[:, k, :],
                                   start=(k == 0), stop=(k == DC - 1))
                mm.then_inc(s["h_mm"], 1)

            def light_out(j, t):
                if t == 3:
                    pe.wait_ge(s["side_out"], TG * j + 1)
                for f in range(LIGHT // P):
                    mm = pe.matmul(ps[:, 5 + (t + 2) % 3, :], hT[:, f, t * P:(t + 1) * P], w2[:, f, :],
                                   start=(f == 0), stop=(f == LIGHT // P - 1))
                mm.then_inc(s["side_mm"], 1)

            def turn(i, prev, cur, nxt, nxt2):
                for st in range(UNITS):
                    if cur:
                        scores(i, st)
                    if st == 0 and cur and not gate:
                        query(i, DC - 1, range(DC))
                    if st in (1, 2) and nxt:
                        if st == 1:
                            pe.wait_ge(s["xn"], TG * (i + 2))
                            reached(pe, s["q_out"], DC * i + (4 if gate else 3))
                            if prev and not gate:
                                reached(pe, s["side_out"], TG * (i - 1))
                        else:
                            pe.wait_ge(s["xnT_dve"], 2 * (i + 1) + 1)
                        transposes(xn, 2 * st - 2, 6, s["xnT_mm"])
                        if st == 2:
                            pe.wait_ge(s["xnT_act"], 2 * (i + 1) + 1)
                        transposes(xn, 2 * st - 1, 7, s["xnT_mm"])
                    if prev:
                        j = i - 1
                        if st == 3:
                            project(j, 0)
                        if st == 4:
                            project(j, 1)
                            project(j, 2)
                        if st == 5:
                            project(j, 3)
                    if st in (7, 8) and nxt:
                        query(i + 1, st - 7, range(DC))
                    if st in (9, 10) and nxt:
                        query(i + 1, 2, range(2) if st == 9 else range(2, DC))
                    if prev:
                        if st == 11:
                            pe.wait_ge(s["z"], TG * i)
                            transposes(z, 0, 5, s["z_mm"])
                            if nxt:
                                pe.wait_ge(s["q_out"], DC * (i + 1) + 1)
                            transposes(z, 1, 6, s["z_mm"])
                        if st == 12:
                            pe.wait_ge(s["zT_dve"], 2 * j + 1)
                            transposes(z, 2, 5, s["z_mm"])
                            pe.wait_ge(s["zT_act"], 2 * j + 1)
                            transposes(z, 3, 6, s["z_mm"])
                    if st in (13, 15) and nxt and gate:
                        query(i + 1, DC - 1, range(2) if st == 13 else range(2, DC))
                    if prev:
                        if st == 13:
                            pe.wait_ge(s["zT_dve"], 2 * j + 2)
                            pe.wait_ge(s["zT_act"], 2 * j + 2)
                        if gate:
                            if st == 13:
                                for k in range(DC):
                                    mm = pe.matmul(ps[k * E:(k + 1) * E, 5, :], wg[:, k, :], zT[:, k, :],
                                                   start=True, stop=True)
                                mm.then_inc(s["part_mm"], 1)
                            if st == 14:
                                pe.wait_ge(s["part"], i)
                                for t in range(TG):
                                    mm = pe.transpose(ps[:, 5, t * P:(t + 1) * P], part[:, t * P:(t + 1) * P],
                                                      ident[:])
                                mm.then_inc(s["side_mm"], 1)
                        else:
                            if st in (13, 14):
                                hidden(j, st - 13)
                    if st < 2 and prev:
                        p_transposes(i - 1, UNITS - 2 + st)
                    if st >= 2 and cur:
                        p_transposes(i, st - 2)
                    if st == 2 and prev:
                        values(i - 1, GROUPS - 1)
                    if st in (6, 10, 14) and cur:
                        values(i, st // TG - 1)
                    if st == 15 and prev and not gate:
                        pe.wait_ge(s["h_out"], (LIGHT // P) * i)
                        if nxt:
                            pe.wait_ge(s["q_out"], DC * (i + 1) + 3)
                        for t in range(TG):
                            light_out(j, t)

            turns(pe, turn)


def expert_slots_phase(nc, a, scr, c):
    BIG = 65536.0
    W = P + 2
    with ExitStack() as ctx:
        def sb(name, shape, dt=F32):
            return ctx.enter_context(nc.sbuf_tensor(f"r_{name}", shape, dt))

        prob, gt, eq, run = (sb(n, [P, NT, E]) for n in ("prob", "gt", "eq", "run"))
        restart = sb("restart", [P, NT, E])
        edge, z, rz, need, ws = (sb(n, [P, NT]) for n in ("edge", "z", "rz", "need", "ws"))
        selT, count = sb("selT", [NT, E, P]), sb("count", [NT, E, P])
        restartT = sb("restartT", [NT, E, P])
        before = sb("before", [NT, NT + 1])
        base, upto = sb("base", [NT + 1, E]), sb("upto", [NT + 1, E])
        table = sb("table", [NT + 1, E, W])
        slots = sb("slots", [NT + 1, CAP])
        ge, hot = sb("ge", [NT + 1, 2, CAP]), sb("hot", [NT + 1, 2, CAP])
        slot_no = sb("slot_no", [P, CC])
        junk = sb("junk", [P, CC, P])
        rank = sb("rank", [P, E, CC])
        found = sb("found", [P, E, CC, 2])
        zero = sb("zero", [P, CC, XW])
        ps = c["ps"]
        s = Sems(nc, ctx, "r", "made shifted exped step weights selected selT_mm counted based tabled "
                               "ge_made hot_made hot_mm looked_up stored")
        block = ctx.enter_context(nc.Block())

        @block.gpsimd
        def _(pool):
            pool.memset(before[:], 1.0).then_inc(s["made"], 1)
            pool.wait_ge(s["made"], 1)
            pool.affine_select(out=before[:], in_=before[:], compare_op=ALU.is_gt, fill=0.0, base=0,
                               pattern=[[1, NT + 1]], channel_multiplier=-1).then_inc(s["made"], 1)
            pool.iota(slots[:], [[1, CAP]], base=0, channel_multiplier=0,
                      allow_small_or_imprecise_dtypes=True).then_inc(s["made"], 1)
            pool.iota(slot_no[:], [[P, CC]], base=0, channel_multiplier=1,
                      allow_small_or_imprecise_dtypes=True).then_inc(s["made"], 1)
            pool.iota(table[:, :, P], [[0, E]], base=0, channel_multiplier=P,
                      allow_small_or_imprecise_dtypes=True).then_inc(s["made"], 1)
            pool.memset(table[:, :, P + 1], 0.0).then_inc(s["made"], 1)
            pool.wait_ge(s["made"], 6)
            pool.memset(zero[:], 0.0).then_inc(s["made"], 1)
            pool.wait_ge(s["made"], 7)
            pool.memset(table[NT:NT + 1, :, P + 1], 1.0).then_inc(s["made"], 1)
            pool.wait_ge(s["made"], 8)
            pool.memset(table[NT:NT + 1, :, 0:P], BIG).then_inc(s["made"], 1)

        @block.sync
        def _(sp):
            sp.wait_ge(s["made"], 9)
            sp.dma_start(scr["xw"][NTOK:NTOK + CAP, :].rearrange("(c p) d -> p c d", p=P),
                         zero[:]).then_inc(s["stored"], 16)
            sp.dma_start(scr["x1"][NTOK:NTOK + CAP, :].rearrange("(c p) d -> p c d", p=P),
                         zero[:, :, 0:D]).then_inc(s["stored"], 16)
            sp.wait_ge(s["weights"], 1)
            sp.dma_start(scr["xw"][0:NTOK, D:XW].rearrange("(t p) e -> p t e", p=P),
                         prob[:]).then_inc(s["stored"], 16)
            sp.wait_ge(s["stored"], 48)

        @block.scalar
        def _(act):
            act.wait_ge(s["shifted"], 1)
            act.activation(prob[:], prob[:], ACT.Exp).then_inc(s["exped"], 1)
            act.activation(edge[:], edge[:], ACT.Exp).then_inc(s["exped"], 1)

        @block.vector
        def _(dve):
            steps = [0]

            def link(op):
                steps[0] += 1
                op.then_inc(s["step"], 1)
                dve.wait_ge(s["step"], steps[0])

            def by_tile(v):
                return v[:].unsqueeze(2).to_broadcast([P, NT, E])

            logits = c["logits"][:].rearrange("p (t e) -> p t e", e=E)
            top8 = c["top8"][:].rearrange("p (t k) -> p t k", k=TOPK)
            dve.memset(restart[:], 1.0)
            dve.memset(restartT[:], 1.0)
            dve.tensor_tensor(edge[:], top8[:, :, TOPK - 1], top8[:, :, 0], ALU.subtract).then_inc(s["step"], 1)
            link(dve.memset(upto[:], 2 * BIG))
            steps[0] += 1
            dve.wait_ge(s["step"], steps[0])
            dve.tensor_tensor(prob[:], logits, top8[:, :, 0].unsqueeze(2).to_broadcast([P, NT, E]),
                              ALU.subtract).then_inc(s["shifted"], 1)
            link(dve.memset(restart[:, :, 0:1], 0.0))
            link(dve.memset(restartT[:, :, 0:1], 0.0))
            dve.wait_ge(s["exped"], 2)
            link(dve.tensor_reduce(z[:], prob[:], AX, ALU.add))
            link(dve.reciprocal(rz[:], z[:]))
            link(dve.tensor_tensor(prob[:], prob[:], by_tile(rz), ALU.mult))
            link(dve.tensor_tensor(edge[:], edge[:], rz[:], ALU.mult))
            link(dve.tensor_tensor(gt[:], prob[:], by_tile(edge), ALU.is_gt))
            link(dve.tensor_tensor(eq[:], prob[:], by_tile(edge), ALU.is_equal))
            link(dve.tensor_reduce(z[:], gt[:], AX, ALU.add))
            link(dve.tensor_scalar(need[:], z[:], -1.0, float(TOPK), ALU.mult, ALU.add))
            link(dve.tensor_tensor_scan(run[:].rearrange("p t e -> p (t e)"),
                                        restart[:].rearrange("p t e -> p (t e)"),
                                        eq[:].rearrange("p t e -> p (t e)"), 0.0, ALU.mult, ALU.add))
            link(dve.tensor_tensor(run[:], run[:], by_tile(need), ALU.is_le))
            link(dve.tensor_tensor(eq[:], run[:], eq[:], ALU.mult))
            dve.tensor_tensor(gt[:], gt[:], eq[:], ALU.add).then_inc(s["selected"], 1)
            dve.wait_ge(s["selected"], 1)
            link(dve.tensor_tensor(prob[:], prob[:], gt[:], ALU.mult))
            link(dve.tensor_reduce(ws[:], prob[:], AX, ALU.add))
            link(dve.reciprocal(ws[:], ws[:]))
            dve.tensor_tensor(prob[:], prob[:], by_tile(ws), ALU.mult).then_inc(s["weights"], 1)
            for b in range(8):
                dve.wait_ge(s["selT_mm"], b + 1)
                op = dve.tensor_copy(selT[:, 4 * b:4 * b + 4, :].rearrange("p e n -> p (e n)"), ps[0:NT, b, :])
                op.then_inc(s["step"], 1)
            steps[0] += 8
            dve.wait_ge(s["step"], steps[0])
            dve.tensor_tensor_scan(count[:].rearrange("p e n -> p (e n)"),
                                   restartT[:].rearrange("p e n -> p (e n)"),
                                   selT[:].rearrange("p e n -> p (e n)"), 0.0, ALU.mult,
                                   ALU.add).then_inc(s["counted"], 1)
            dve.wait_ge(s["based"], 1)
            link(dve.tensor_copy(base[:], ps[0:NT + 1, 0, 0:E]))
            link(dve.tensor_tensor(upto[0:NT, :], base[0:NT, :], count[:, :, P - 1], ALU.add))
            dve.wait_ge(s["made"], 9)
            dve.tensor_tensor(table[0:NT, :, 0:P], count[:], base[0:NT, :].unsqueeze(2).to_broadcast([NT, E, P]),
                              ALU.add).then_inc(s["tabled"], 1)

            def one_hot(e, q):
                dve.tensor_scalar(ge[:, q, :], slots[:], base[:, bass.ds(e, 1)], None,
                                  ALU.is_ge).then_inc(s["ge_made"], 1)
                dve.wait_ge(s["ge_made"], e + 1)
                dve.scalar_tensor_tensor(hot[:, q, :], slots[:], upto[:, bass.ds(e, 1)], ge[:, q, :],
                                         ALU.is_lt, ALU.mult).then_inc(s["hot_made"], 1)

            def look_up(e, q):
                dve.wait_ge(s["hot_mm"], e + 1)
                dve.wait_ge(s["looked_up"], e)
                for n in range(CC):
                    bank, at = 2 * q + n // 2, (n % 2) * W
                    dve.tensor_scalar(junk[:, n, :], ps[:, bank, at:at + P], slot_no[:, n:n + 1], 0.0, ALU.is_le, ALU.add,
                                      accum_out=rank[:, bass.ds(e, 1), n])
                dve.tensor_copy(
                    found[:, bass.ds(e, 1), :, :].rearrange("p o (b n) w -> p (o b) n w", b=2),
                    ps[:, 2 * q:2 * q + 2, 0:2 * W].rearrange("p b (n w) -> p b n w", w=W)[:, :, :, P:W],
                ).then_inc(s["looked_up"], 1)

            one_hot(0, 0)
            with dve.Fori(0, E // 2 - 1) as j:
                one_hot(2 * j + 1, 1)
                look_up(2 * j, 0)
                one_hot(2 * j + 2, 0)
                look_up(2 * j + 1, 1)
            one_hot(E - 1, 1)
            look_up(E - 2, 0)
            look_up(E - 1, 1)
            dve.wait_ge(s["looked_up"], E)
            link(dve.tensor_tensor(rank[:], rank[:], found[:, :, :, 0], ALU.add))
            link(dve.tensor_tensor(found[:, :, :, 1], found[:, :, :, 1],
                                   slot_no[:].unsqueeze(1).to_broadcast([P, E, CC]), ALU.mult))
            link(dve.tensor_tensor(rank[:], rank[:], found[:, :, :, 1], ALU.add))
            dve.tensor_copy(c["expert_rows"][:].rearrange("p (e n) -> p e n", n=CC), rank[:])

        @block.tensor
        def _(pe):
            pe.wait_ge(s["selected"], 1)
            for e in range(E):
                mm = pe.transpose(ps[0:NT, e // 4, (e % 4) * P:(e % 4 + 1) * P], gt[:, :, e], c["ident"][:])
                if e % 4 == 3:
                    mm.then_inc(s["selT_mm"], 1)
            pe.wait_ge(s["counted"], 1)
            pe.wait_ge(s["made"], 9)
            pe.matmul(ps[0:NT + 1, 0, 0:E], before[:], count[:, :, P - 1], start=True,
                      stop=True).then_inc(s["based"], 1)
            pe.wait_ge(s["tabled"], 1)

            def look_up(e, q, first):
                pe.wait_ge(s["hot_made"], e + 1)
                if not first:
                    pe.wait_ge(s["looked_up"], e - 1)
                for n in range(CC):
                    bank, at = 2 * q + n // 2, (n % 2) * W
                    mm = pe.matmul(ps[:, bank, at:at + W], hot[:, q, n * P:(n + 1) * P],
                                   table[:, bass.ds(e, 1), :].rearrange("p o w -> p (o w)"), start=True, stop=True)
                mm.then_inc(s["hot_mm"], 1)

            look_up(0, 0, True)
            look_up(1, 1, True)
            with pe.Fori(1, E // 2) as j:
                look_up(2 * j, 0, False)
                look_up(2 * j + 1, 1, False)


def expert_phase(nc, a, scr, c):
    with ExitStack() as ctx:
        def sb(name, shape, dt=F32):
            return ctx.enter_context(nc.sbuf_tensor(f"e_{name}", shape, dt))

        wgu_in, wd_in = sb("wgu_in", [P, DC, 2 * F]), sb("wd_in", [P, FC, D])
        wgu = [[sb(f"wgu_{part}{q}", [P, DC, 2 * F], F32R) for part in ("high", "low")] for q in range(2)]
        wd = [[sb(f"wd_{part}{q}", [P, FC, D], F32R) for part in ("high", "low")] for q in range(2)]
        idx = [sb(f"idx{q}", [P, CC], I32) for q in range(2)]
        put_idx = sb("put_idx", [P, CC], I32)
        xe = [sb(f"xe{q}", [P, CC, XW]) for q in range(2)]
        xT = [[sb(f"xT_{part}{q}", [P, DC, CAP], F32R) for part in ("high", "low")] for q in range(2)]
        weight = [sb(f"weight{q}", [P, CC]) for q in range(2)]
        y = [sb(f"y{q}", [P, CC, D]) for q in range(2)]
        sig = sb("sig", [P, 2, CAP])
        h = sb("h", [P, CAP])
        hT = [sb(f"hT_{part}", [P, FC, CAP], F32R) for part in ("high", "low")]
        one, tick = sb("one", [P, 1]), sb("tick", [P, 2, CC + 1])
        ps = c["ps"]
        s = Sems(nc, ctx, "e", "ready wgu_in wd_in idx put_idx gathered0 gathered1 scattered x_mm x_high xT weight gu_mm silu "
                               "h h_high hT d_mm y wgu_high wgu_low wd_high wd_low")
        block = ctx.enter_context(nc.Block())

        def turns(engine, body):
            body(0, True, False)
            with engine.Fori(1, E // 2 - 1) as j:
                body(j, False, False)
            body(E // 2 - 1, False, True)

        def arrivals(e, q):
            return (e - q) // 2 + 1

        @block.sync
        def _(sp):
            def load(e):
                gate_up = a["gate_upT"][bass.ds(e * D, D), :].rearrange("(k p) f -> p k f", p=P)
                down = a["downT"][bass.ds(e * F, F), :].rearrange("(k p) d -> p k d", p=P)
                reached(sp, s["wgu_low"], DC * e)
                sp.dma_start(wgu_in[:], gate_up).then_inc(s["wgu_in"], 16)
                reached(sp, s["wd_low"], FC * e)
                sp.dma_start(wd_in[:], down).then_inc(s["wd_in"], 16)

            load(0)
            load(1)

            def turn(j, first, last):
                if not last:
                    load(2 * j + 2)
                    load(2 * j + 3)

            turns(sp, turn)

        @block.gpsimd
        def _(pool):
            pool.memset(one[:], 1.0).then_inc(s["ready"], 1)
            pool.wait_ge(s["ready"], 1)

            def stand(q, n):
                pool.tensor_tensor(tick[:, q, n:n + 1], one[:], one[:], ALU.add)

            def gather(e, q, first):
                if not first:
                    pool.wait_ge(s["x_mm"], DC * (e - 1))
                    pool.wait_ge(s["weight"], e - 1)
                stand(q, CC)
                pool.tensor_copy(idx[q][:], c["expert_rows"][:, bass.ds(CC * e, CC)]).then_inc(s["idx"], 1)
                pool.wait_ge(s["idx"], e + 1)
                stand(q, CC)
                for n in range(CC):
                    pool.indirect_dma_start(
                        out=xe[q][:, n, :], out_offset=None, in_=scr["xw"][:, :],
                        in_offset=bass.IndirectOffsetOnAxis(ap=idx[q][:, n:n + 1], axis=0),
                    ).then_inc(s[f"gathered{q}"], 16)

            def scatter(e, q):
                reached(pool, s["scattered"], 16 * CC * e)
                stand(q, CC)
                pool.tensor_copy(put_idx[:], c["expert_rows"][:, bass.ds(CC * e, CC)]).then_inc(s["put_idx"], 1)
                pool.wait_ge(s["put_idx"], e + 1)
                for n in range(CC):
                    pool.wait_ge(s["y"], CC * e + n + 1)
                    stand(q, n)
                    pool.indirect_dma_start(
                        out=scr["x1"][:, :], out_offset=bass.IndirectOffsetOnAxis(ap=put_idx[:, n:n + 1], axis=0),
                        in_=y[q][:, n, :], in_offset=None, compute_op=ALU.add).then_inc(s["scattered"], 16)

            def low_weights(e, q):
                reached(pool, s["d_mm"], CC * (e - 1))
                pool.wait_ge(s["wgu_high"], DC * e + DC)
                pool.tensor_tensor(wgu[q][1][:, DC - 1, :], wgu_in[:, DC - 1, :],
                                   wgu[q][0][:, DC - 1, :].bitcast(F32), ALU.subtract).then_inc(s["wgu_low"], 1)
                for f in range(FC):
                    pool.wait_ge(s["wd_high"], FC * e + f + 1)
                    pool.tensor_tensor(wd[q][1][:, f, :], wd_in[:, f, :], wd[q][0][:, f, :].bitcast(F32),
                                       ALU.subtract).then_inc(s["wd_low"], 1)

            gather(0, 0, True)
            low_weights(0, 0)

            def turn(j, first, last):
                gather(2 * j + 1, 1, first)
                low_weights(2 * j + 1, 1)
                scatter(2 * j, 0)
                if not last:
                    gather(2 * j + 2, 0, False)
                    low_weights(2 * j + 2, 0)
                scatter(2 * j + 1, 1)

            turns(pool, turn)
            pool.wait_ge(s["scattered"], 16 * CC * E)

        @block.vector
        def _(dve):
            def transposed(e, q, chunks):
                for k in chunks:
                    dve.wait_ge(s["x_mm"], DC * e + k + 1)
                    high_of(dve, xT[q][0][:, k, :], ps[:, 4 + k % 2, :]).then_inc(s["x_high"], 1)
                    dve.wait_ge(s["x_high"], DC * e + k + 1)
                    dve.tensor_tensor(xT[q][1][:, k, :], ps[:, 4 + k % 2, :], xT[q][0][:, k, :].bitcast(F32),
                                      ALU.subtract).then_inc(s["xT"], 1)
            def token_weights(e, q):
                dve.wait_ge(s[f"gathered{q}"], arrivals(e, q) * 16 * CC)
                dve.tensor_scalar(weight[q][:].unsqueeze(2), xe[q][:, :, bass.ds(D + e, 1)], 1.0, None,
                                  ALU.mult).then_inc(s["weight"], 1)

            def split_gate_up(e, q, k):
                dve.wait_ge(s["wgu_in"], 16 * e + 16)
                high_of(dve, wgu[q][0][:, k, :], wgu_in[:, k, :]).then_inc(s["wgu_high"], 1)
                if k < DC - 1:
                    dve.wait_ge(s["wgu_high"], DC * e + k + 1)
                    dve.tensor_tensor(wgu[q][1][:, k, :], wgu_in[:, k, :], wgu[q][0][:, k, :].bitcast(F32),
                                      ALU.subtract).then_inc(s["wgu_low"], 1)

            def split_weights(e, q, step):
                reached(dve, s["d_mm"], CC * (e - 1))
                if step == 0:
                    split_gate_up(e, q, 0)
                    split_gate_up(e, q, 1)
                elif step == 1:
                    split_gate_up(e, q, 2)
                    split_gate_up(e, q, 3)
                else:
                    dve.wait_ge(s["wd_in"], 16 * e + 16)
                    for f in range(FC):
                        high_of(dve, wd[q][0][:, f, :], wd_in[:, f, :]).then_inc(s["wd_high"], 1)

            for step in range(3):
                split_weights(0, 0, step)
            transposed(0, 0, range(DC))
            token_weights(0, 0)

            def expert(e, q, first, last):
                for f in range(FC):
                    b = 2 * ((FC * q + f) % 2)
                    dve.wait_ge(s["silu"], FC * e + f + 1)
                    reached(dve, s["hT"], FC * e + f)
                    dve.tensor_tensor(h[:], sig[:, (FC * q + f) % 2, :], ps[:, b + 1, :], ALU.mult).then_inc(s["h"], 1)
                    dve.wait_ge(s["h"], FC * e + f + 1)
                    high_of(dve, hT[0][:, f, :], h[:]).then_inc(s["h_high"], 1)
                    dve.wait_ge(s["h_high"], FC * e + f + 1)
                    dve.tensor_tensor(hT[1][:, f, :], h[:], hT[0][:, f, :].bitcast(F32),
                                      ALU.subtract).then_inc(s["hT"], 1)
                    if not last and f == 2:
                        transposed(e + 1, 1 - q, (2, 3))
                    if not last and f == 1:
                        transposed(e + 1, 1 - q, (0, 1))
                    if not last:
                        split_weights(e + 1, 1 - q, f)
                if not last:
                    token_weights(e + 1, 1 - q)

            def turn(j, first, last):
                expert(2 * j, 0, first, False)
                expert(2 * j + 1, 1, first, last)

            turns(dve, turn)

        @block.scalar
        def _(act):
            def expert(e, q, first, last):
                for f in range(FC):
                    b = 2 * ((FC * q + f) % 2)
                    act.wait_ge(s["gu_mm"], FC * e + f + 1)
                    reached(act, s["h"], FC * e + f - 1)
                    act.activation(sig[:, (FC * q + f) % 2, :], ps[:, b, :], ACT.Silu).then_inc(s["silu"], 1)
                reached(act, s["scattered"], 16 * CC * (e - 1))
                act.wait_ge(s["weight"], e + 1)
                for n in range(CC):
                    act.wait_ge(s["d_mm"], CC * e + n + 1)
                    act.activation(y[q][:, n, :], ps[:, 6 + n % 2, :], ACT.Copy,
                                   scale=weight[q][:, n:n + 1]).then_inc(s["y"], 1)

            def turn(j, first, last):
                expert(2 * j, 0, first, False)
                expert(2 * j + 1, 1, first, last)

            turns(act, turn)

        @block.tensor
        def _(pe):
            def transposes(e, q, chunks, start):
                pe.wait_ge(s[f"gathered{q}"], arrivals(e, q) * 16 * CC)
                for k in chunks:
                    if not (start and k < 2):
                        pe.wait_ge(s["xT"], DC * e + k - 1)
                    for n in range(CC):
                        mm = pe.transpose(ps[:, 4 + k % 2, n * P:(n + 1) * P],
                                          xe[q][:, n, k * P:(k + 1) * P], c["ident"][:])
                    mm.then_inc(s["x_mm"], 1)

            transposes(0, 0, range(DC), True)

            def expert(e, q, first, last):
                pe.wait_ge(s["wgu_low"], DC * e + DC)
                pe.wait_ge(s["xT"], DC * e + DC)
                for f in range(FC):
                    b = 2 * ((FC * q + f) % 2)
                    if not (first and q == 0 and f < 2):
                        pe.wait_ge(s["h"], FC * e + f - 1)
                    for part in range(2):
                        for k in range(DC):
                            col = part * F + f * P
                            mm = product(pe, ps[:, b + part, :], [w[:, k, col:col + P] for w in wgu[q]],
                                         [v[:, k, :] for v in xT[q]], k == 0, k == DC - 1)
                    mm.then_inc(s["gu_mm"], 1)
                    if not last and f >= 1:
                        transposes(e + 1, 1 - q, (2 * f - 2, 2 * f - 1), False)
                pe.wait_ge(s["wd_low"], FC * e + FC)
                for n in range(CC):
                    if not (first and q == 0 and n < 2):
                        pe.wait_ge(s["y"], CC * e + n - 1)
                    for f in range(FC):
                        if n == 0:
                            pe.wait_ge(s["hT"], FC * e + f + 1)
                        mm = product(pe, ps[:, 6 + n % 2, :], [v[:, f, n * P:(n + 1) * P] for v in hT],
                                     [w[:, f, :] for w in wd[q]], f == 0, f == FC - 1)
                    mm.then_inc(s["d_mm"], 1)

            def turn(j, first, last):
                expert(2 * j, 0, first, False)
                expert(2 * j + 1, 1, first, last)

            turns(pe, turn)


def routing_phase(nc, a, scr, c):
    R = P // B
    C = SEQ // R
    LOGK = math.log(EFF_K)
    MADE = 3 + 3 * B + 4
    with ExitStack() as ctx:
        def sb(name, shape, dt=F32):
            return ctx.enter_context(nc.sbuf_tensor(f"d_{name}", shape, dt))

        flat = sb("flat", [NT, P])
        sco, sbv, ex = sb("sco", [P, C]), sb("sbv", [P, C]), sb("ex", [P, C])
        top, wide, wideT, smax = sb("top", [P, 1]), sb("wide", [P, R]), sb("wideT", [P, R]), sb("smax", [P, 1])
        na, nm, part, lse = (sb(n, [P, 1]) for n in ("na", "nm", "part", "lse"))
        same, earlier, ones = sb("same", [P, P]), sb("earlier", [P, P]), sb("ones", [P, C])
        pick = sb("pick", [P, B, P])
        u, below, equal, run, sel, pos = (sb(n, [P, C]) for n in ("u", "below", "equal", "run", "sel", "pos"))
        edge, bit, cand, few = (sb(n, [P, 1], I32) for n in ("edge", "bit", "cand", "few"))
        cnt, need, pre = (sb(n, [P, 1]) for n in ("cnt", "need", "pre"))
        batch = sb("batch", [P, B])
        row, col = sb("row", [P, 1]), sb("col", [P, C])
        vals = sb("vals", [P, C, 2 * B], BF16)
        slots = sb("slots", [P, ROUTED])
        hot = sb("hot", [P, 4, ROUTED], BF16)
        found, rows_f = sb("found", [2 * B, ROUTED]), sb("rows_f", [P, B, CC])
        ps = c["ps"]
        s = Sems(nc, ctx, "d", "w_in made flat_mm flat flat_out s_in step ready shifted exped summed logged na "
                               "cand counted count_mm shift edge pre_mm hot hot_mm found found_mm")
        block = ctx.enter_context(nc.Block())

        @block.sync
        def _(sp):
            sp.dma_start(c["hw1"][:], a["heavy_w1"].rearrange("(k p) f -> p k f", p=P)).then_inc(c["hw_in"], 16)
            sp.wait_ge(s["flat"], 1)
            sp.dma_start(scr["scores"].rearrange("(t p) -> t p", p=P), flat[:]).then_inc(s["flat_out"], 16)
            sp.wait_ge(s["flat_out"], 16)
            sp.dma_start(sco[:], scr["scores"].rearrange("(q j) -> q j", j=C)).then_inc(s["s_in"], 16)
            sp.dma_start(c["hw2"][:], a["heavy_w2"].rearrange("(f p) d -> p f d", p=P)).then_inc(c["hw_in"], 16)
            sp.dma_start(c["hb2"][:], a["heavy_b2"].partition_broadcast(P)).then_inc(c["hw_in"], 16)
            with nc.allow_non_contiguous_dma(reason="biases and scales by partition"):
                sp.dma_start(c["hb1"][:], a["heavy_b1"].rearrange("(k p) -> p k", p=P)).then_inc(c["hw_in"], 16)
                sp.dma_start(c["hgam"][:], a["heavy_gamma"].rearrange("(k p) -> p k", p=P)).then_inc(c["hw_in"], 16)

        @block.gpsimd
        def _(pool):
            n = [0]

            def made(op):
                n[0] += 1
                op.then_inc(s["made"], 1)
                pool.wait_ge(s["made"], n[0])

            made(pool.memset(same[:], 0.0))
            made(pool.memset(batch[:], 0.0))
            made(pool.memset(pick[:], 0.0))
            for b in range(B):
                made(pool.memset(same[R * b:R * (b + 1), R * b:R * (b + 1)], 1.0))
                made(pool.memset(batch[R * b:R * (b + 1), b:b + 1], 1.0))
                made(pool.memset(pick[R * b:R * b + 1, b, :], 1.0))
            made(pool.affine_select(out=earlier[:], in_=same[:], compare_op=ALU.is_gt, fill=0.0, base=0,
                                    pattern=[[1, P]], channel_multiplier=-1))
            made(pool.iota(row[:], [[0, 1]], base=0, channel_multiplier=1, allow_small_or_imprecise_dtypes=True))
            made(pool.iota(col[:], [[1, C]], base=0, channel_multiplier=0, allow_small_or_imprecise_dtypes=True))
            made(pool.iota(slots[:], [[1, ROUTED]], base=0, channel_multiplier=0,
                           allow_small_or_imprecise_dtypes=True))
            assert n[0] == MADE


        @block.scalar
        def _(act):
            act.preload_act_table_set("natural_log_exp_and_others")

            def turn(i):
                act.wait_ge(s["shifted"], i + 1)
                act.activation(ex[:], sbv[:], ACT.Exp, bias=nm[:], accum_out=part[:]).then_inc(s["exped"], 1)
                act.wait_ge(s["summed"], i + 1)
                act.activation(lse[:], ps[:, 1, 0:1], ACT.Ln).then_inc(s["logged"], 1)

            with act.Fori(0, ITERS - 1) as i:
                turn(i)

        @block.tensor
        def _(pe):
            pe.transpose(ps[0:NT, 0, 0:P], c["scores"][:], c["ident"][:]).then_inc(s["flat_mm"], 1)
            pe.wait_ge(s["made"], MADE)
            with pe.Fori(0, ITERS - 1) as i:
                pe.wait_ge(s["exped"], i + 1)
                pe.matmul(ps[:, 1, 0:1], same[:], part[:], start=True, stop=True).then_inc(s["summed"], 1)
            with pe.Fori(0, 31) as i:
                pe.wait_ge(s["counted"], i + 1)
                pe.matmul(ps[:, 2, 0:1], same[:], cnt[:], start=True, stop=True).then_inc(s["count_mm"], 1)
            pe.wait_ge(s["counted"], 32)
            pe.matmul(ps[:, 2, 0:1], same[:], cnt[:], start=True, stop=True).then_inc(s["count_mm"], 1)
            pe.wait_ge(s["ready"], 1)
            pe.matmul(ps[:, 3, 0:1], earlier[:], run[:, C - 1:C], start=True, stop=True).then_inc(s["pre_mm"], 1)
            pe.wait_ge(s["ready"], 2)
            pe.matmul(ps[:, 3, 0:1], earlier[:], run[:, C - 1:C], start=True, stop=True).then_inc(s["pre_mm"], 1)
            for b in range(B):
                mm = pe.matmul(ps[:, 4, b:b + 1], pick[:, b, :], na[:], start=True, stop=True)
            mm.then_inc(s["pre_mm"], 1)
            for j in range(C):
                pe.wait_ge(s["hot"], j + 1)
                pe.matmul(ps[0:2 * B, 5, :], vals[:, j, :], hot[:, j % 4, :], start=(j == 0),
                          stop=(j == C - 1)).then_inc(s["hot_mm"], 1)
            pe.wait_ge(s["found"], 1)
            for n in range(CC):
                mm = pe.transpose(ps[:, 6, n * 2 * B:(n + 1) * 2 * B], found[:, n * P:(n + 1) * P],
                                  c["ident"][0:2 * B, 0:2 * B])
            mm.then_inc(s["found_mm"], 1)

        @block.vector
        def _(dve):
            steps = [0]

            def link(op):
                steps[0] += 1
                op.then_inc(s["step"], 1)
                dve.wait_ge(s["step"], steps[0])

            dve.wait_ge(s["flat_mm"], 1)
            dve.tensor_copy(flat[:], ps[0:NT, 0, 0:P]).then_inc(s["flat"], 1)
            link(dve.memset(ones[:], 1.0))
            link(dve.memset(na[:], math.log(SEQ) - LOGK))
            link(dve.memset(edge[:].bitcast(F32), 0.0))
            link(dve.memset(bit[:].bitcast(F32), 2.0))
            dve.wait_ge(s["s_in"], 16)
            link(dve.tensor_reduce(top[:], sco[:], AX, ALU.max))
            link(dve.tensor_scalar(wide[:], ones[:, 0:R], top[:], None, ALU.mult))
            link(dve.transpose(wideT[:], wide[:]))
            link(dve.tensor_reduce(smax[:], wideT[:], AX, ALU.max))
            with dve.Fori(0, ITERS - 1) as i:
                dve.wait_ge(s["na"], i)
                dve.tensor_scalar(nm[:], na[:], smax[:], -1.0, ALU.min, ALU.mult)
                dve.tensor_scalar(sbv[:], sco[:], na[:], None, ALU.min).then_inc(s["shifted"], 1)
                dve.wait_ge(s["logged"], i + 1)
                dve.tensor_scalar(na[:], lse[:], nm[:], LOGK, ALU.subtract, ALU.subtract).then_inc(s["na"], 1)
            dve.wait_ge(s["na"], ITERS - 1)
            link(dve.tensor_scalar(u[:], sco[:], na[:], -1.0, ALU.subtract, ALU.mult))
            link(dve.tensor_scalar(u[:], u[:], 0.0, 104.0, ALU.max, ALU.min))
            with dve.Fori(0, 31) as i:
                dve.wait_ge(s["edge"], i)
                dve.tensor_tensor(cand[:], edge[:], bit[:], ALU.bitwise_or).then_inc(s["cand"], 1)
                dve.wait_ge(s["cand"], i + 1)
                dve.tensor_scalar(below[:], u[:], cand[:].bitcast(F32), 0.0, ALU.is_lt, ALU.add,
                                  accum_out=cnt[:]).then_inc(s["counted"], 1)
                dve.tensor_scalar(bit[:], bit[:], 1, None, ALU.logical_shift_right).then_inc(s["shift"], 1)
                dve.wait_ge(s["count_mm"], i + 1)
                dve.tensor_scalar(few[:], ps[:, 2, 0:1], float(ROUTED), None, ALU.is_lt).then_inc(s["shift"], 1)
                dve.wait_ge(s["shift"], 2 * i + 2)
                dve.tensor_scalar(wide[:, 0:1], ones[:, 0:1], 1.0, None, ALU.mult)
                dve.copy_predicated(edge[:], few[:], cand[:]).then_inc(s["edge"], 1)
            dve.wait_ge(s["edge"], 31)
            dve.tensor_scalar(below[:], u[:], edge[:].bitcast(F32), 0.0, ALU.is_lt, ALU.add,
                              accum_out=cnt[:]).then_inc(s["counted"], 1)
            link(dve.tensor_scalar(equal[:], u[:], edge[:].bitcast(F32), None, ALU.is_equal))
            dve.wait_ge(s["count_mm"], 32)
            link(dve.tensor_scalar(need[:], ps[:, 2, 0:1], -1.0, float(ROUTED), ALU.mult, ALU.add))
            dve.tensor_tensor_scan(run[:], ones[:], equal[:], 0.0, ALU.mult, ALU.add).then_inc(s["ready"], 1)
            dve.wait_ge(s["pre_mm"], 1)
            link(dve.tensor_copy(pre[:], ps[:, 3, 0:1]))
            link(dve.tensor_scalar(sel[:], run[:], pre[:], need[:], ALU.add, ALU.is_le))
            link(dve.tensor_tensor(sel[:], sel[:], equal[:], ALU.mult))
            link(dve.tensor_tensor(sel[:], sel[:], below[:], ALU.add))
            dve.tensor_tensor_scan(run[:], ones[:], sel[:], 0.0, ALU.mult, ALU.add).then_inc(s["ready"], 1)
            dve.wait_ge(s["pre_mm"], 2)
            link(dve.tensor_copy(pre[:], ps[:, 3, 0:1]))
            link(dve.tensor_scalar(pos[:], run[:], pre[:], None, ALU.add))
            link(dve.tensor_tensor(pos[:], pos[:], sel[:], ALU.mult))
            link(dve.tensor_scalar(pos[:], pos[:], -1.0, None, ALU.add))
            dve.wait_ge(s["made"], MADE)
            link(dve.tensor_scalar(vals[:, :, 0:B], batch[:].unsqueeze(1).to_broadcast([P, C, B]), row[:], None,
                                   ALU.mult))
            link(dve.tensor_tensor(vals[:, :, B:2 * B], batch[:].unsqueeze(1).to_broadcast([P, C, B]),
                                   col[:].unsqueeze(2).to_broadcast([P, C, B]), ALU.mult))
            for j in range(C):
                if j >= 4:
                    dve.wait_ge(s["hot_mm"], j - 3)
                dve.tensor_scalar(hot[:, j % 4, :], slots[:], pos[:, j:j + 1], None, ALU.is_equal).then_inc(s["hot"], 1)
            dve.wait_ge(s["pre_mm"], 3)
            dve.tensor_copy(c["na"][:], ps[:, 4, 0:B])
            dve.wait_ge(s["hot_mm"], C)
            dve.tensor_copy(found[:], ps[0:2 * B, 5, :]).then_inc(s["found"], 1)
            dve.wait_ge(s["found_mm"], 1)
            got = ps[:, 6, 0:CC * 2 * B].rearrange("p (n w) -> p w n", w=2 * B)
            link(dve.tensor_copy(rows_f[:], got[:, B:2 * B, :]))
            link(dve.scalar_tensor_tensor(rows_f[:], got[:, 0:B, :], float(C), rows_f[:], ALU.mult, ALU.add))
            dve.tensor_copy(c["heavy_rows"][:], rows_f[:])


def heavy_phase(nc, a, scr, c, out):
    RING = 3
    with ExitStack() as ctx:
        def sb(name, shape, dt=F32):
            return ctx.enter_context(nc.sbuf_tensor(f"h_{name}", shape, dt))

        xh = [sb(f"xh{q}", [P, CC, XS]) for q in range(2)]
        xg = sb("xg", [P, CAP])
        xT = [sb(f"xT_{part}", [P, DC, CAP], F32R) for part in ("high", "low")]
        w1 = [sb(f"w1_{part}", [P, RING, DC, P], F32R) for part in ("high", "low")]
        w2 = [sb(f"w2_{part}", [P, RING, D], F32R) for part in ("high", "low")]
        h = sb("h", [P, 2, CAP])
        hT = [sb(f"hT_{part}", [P, 2, CAP], F32R) for part in ("high", "low")]
        y = [sb(f"y{q}", [P, CC, D]) for q in range(2)]
        val, ex, rest, one = (sb(n, [P, CC]) for n in ("val", "ex", "rest", "one"))
        ps = c["ps"]
        s = Sems(nc, ctx, "h", "gathered0 gathered1 scattered x_mm xg x_high xT val ex rest one w_high w1 w2 "
                               "h_mm h h_high hT d_mm yb y")
        block = ctx.enter_context(nc.Block())

        @block.gpsimd
        def _(pool):
            def gather(b):
                if b >= 2:
                    pool.wait_ge(s["x_mm"], DC * (b - 1))
                    pool.wait_ge(s["val"], b - 1)
                for n in range(CC):
                    pool.indirect_dma_start(
                        out=xh[b % 2][:, n, :], out_offset=None, in_=scr["xs"][:, :],
                        in_offset=bass.IndirectOffsetOnAxis(ap=c["heavy_rows"][:, b, n:n + 1], axis=0),
                    ).then_inc(s[f"gathered{b % 2}"], 16)

            gather(0)
            for b in range(B):
                if b + 1 < B:
                    gather(b + 1)
                for f in range(HC):
                    m = HC * b + f
                    pool.wait_ge(s["w_high"], 2 * m + 1)
                    pool.tensor_tensor(w1[1][:, f % RING], c["hw1"][:, :, f * P:(f + 1) * P],
                                       w1[0][:, f % RING].bitcast(F32), ALU.subtract).then_inc(s["w1"], 1)
                for n in range(CC):
                    pool.wait_ge(s["y"], CC * b + n + 1)
                    pool.indirect_dma_start(
                        out=out[:, :], out_offset=bass.IndirectOffsetOnAxis(ap=c["heavy_rows"][:, b, n:n + 1], axis=0),
                        in_=y[b % 2][:, n, :], in_offset=None, compute_op=ALU.add).then_inc(s["scattered"], 16)
            pool.wait_ge(s["scattered"], 16 * CC * B)

        def turns(engine, body):
            body(0, 0, 0)
            body(1, 0, 1)
            with engine.Fori(1, B // 2) as j:
                body(2 * j, j, 0)
                body(2 * j + 1, j, 1)

        @block.vector
        def _(dve):
            dve.wait_ge(c["hw_in"], 80)

            def split_weights(b, f):
                n = HC * b + f
                reached(dve, s["d_mm"], n - RING + 1)
                high_of(dve, w1[0][:, f % RING], c["hw1"][:, :, f * P:(f + 1) * P]).then_inc(s["w_high"], 1)
                high_of(dve, w2[0][:, f % RING, :], c["hw2"][:, f, :]).then_inc(s["w_high"], 1)
                dve.wait_ge(s["w_high"], 2 * n + 2)
                dve.tensor_tensor(w2[1][:, f % RING, :], c["hw2"][:, f, :], w2[0][:, f % RING, :].bitcast(F32),
                                  ALU.subtract).then_inc(s["w2"], 1)

            def batch(b, j, q):
                split_weights(b, 0)
                dve.wait_ge(s[f"gathered{q}"], 16 * CC * (j + 1))
                dve.tensor_scalar(val[:], xh[q][:, :, D], c["na"][:, bass.ds(b, 1)], 0.0, ALU.subtract,
                                  ALU.min).then_inc(s["val"], 1)
                for k in range(DC):
                    dve.wait_ge(s["x_mm"], DC * b + k + 1)
                    reached(dve, s["xT"], DC * b + k)
                    dve.tensor_scalar(xg[:], ps[:, 6 + k % 2, :], c["hgam"][:, k:k + 1], None,
                                      ALU.mult).then_inc(s["xg"], 1)
                    dve.wait_ge(s["xg"], DC * b + k + 1)
                    high_of(dve, xT[0][:, k, :], xg[:]).then_inc(s["x_high"], 1)
                    dve.wait_ge(s["x_high"], DC * b + k + 1)
                    dve.tensor_tensor(xT[1][:, k, :], xg[:], xT[0][:, k, :].bitcast(F32),
                                      ALU.subtract).then_inc(s["xT"], 1)
                dve.wait_ge(s["ex"], b + 1)
                dve.tensor_scalar(rest[:], ex[:], -1.0, 1.0, ALU.mult, ALU.add).then_inc(s["rest"], 1)
                dve.wait_ge(s["rest"], b + 1)
                dve.tensor_tensor(one[:], ex[:], rest[:], ALU.add).then_inc(s["one"], 1)
                for f in range(HC):
                    if f + 1 < HC:
                        split_weights(b, f + 1)
                    n = HC * b + f
                    dve.wait_ge(s["h"], n + 1)
                    reached(dve, s["d_mm"], n - 1)
                    high_of(dve, hT[0][:, f % 2, :], h[:, f % 2, :]).then_inc(s["h_high"], 1)
                    dve.wait_ge(s["h_high"], n + 1)
                    dve.tensor_tensor(hT[1][:, f % 2, :], h[:, f % 2, :], hT[0][:, f % 2, :].bitcast(F32),
                                      ALU.subtract).then_inc(s["hT"], 1)
                dve.wait_ge(s["d_mm"], HC * (b + 1))
                reached(dve, s["scattered"], 16 * CC * b)
                for n in range(CC):
                    dve.tensor_tensor(y[q][:, n, :], ps[:, n, :], c["hb2"][:], ALU.add).then_inc(s["yb"], 1)
                for n in range(CC):
                    dve.wait_ge(s["yb"], CC * b + n + 1)
                    dve.tensor_scalar(y[q][:, n, :], y[q][:, n, :], one[:, n:n + 1], None,
                                      ALU.mult).then_inc(s["y"], 1)

            turns(dve, batch)

        @block.scalar
        def _(act):
            act.wait_ge(c["hw_in"], 80)

            def batch(b, j, q):
                act.wait_ge(s["val"], b + 1)
                reached(act, s["one"], b)
                act.activation(ex[:], val[:], ACT.Exp).then_inc(s["ex"], 1)
                for f in range(HC):
                    n = HC * b + f
                    act.wait_ge(s["h_mm"], n + 1)
                    reached(act, s["hT"], n - 1)
                    act.activation(h[:, f % 2, :], ps[:, 4 + f % 2, :], ACT.Gelu,
                                   bias=c["hb1"][:, f:f + 1]).then_inc(s["h"], 1)

            turns(act, batch)

        @block.tensor
        def _(pe):
            pe.wait_ge(c["hw_in"], 80)

            def batch(b, j, q):
                pe.wait_ge(s[f"gathered{q}"], 16 * CC * (j + 1))
                for k in range(DC):
                    if k >= 2:
                        pe.wait_ge(s["xT"], DC * b + k - 1)
                    for n in range(CC):
                        mm = pe.transpose(ps[:, 6 + k % 2, n * P:(n + 1) * P], xh[q][:, n, k * P:(k + 1) * P],
                                          c["ident"][:])
                    mm.then_inc(s["x_mm"], 1)
                pe.wait_ge(s["xT"], DC * b + DC)

                def hidden(f):
                    n = HC * b + f
                    pe.wait_ge(s["w1"], n + 1)
                    reached(pe, s["h"], n - 1)
                    for k in range(DC):
                        mm = product(pe, ps[:, 4 + f % 2, :], [w[:, f % RING, k, :] for w in w1],
                                     [v[:, k, :] for v in xT], k == 0, k == DC - 1)
                    mm.then_inc(s["h_mm"], 1)

                hidden(0)
                for f in range(HC):
                    if f + 1 < HC:
                        hidden(f + 1)
                    if f == 0:
                        reached(pe, s["yb"], CC * b)
                    pe.wait_ge(s["hT"], HC * b + f + 1)
                    pe.wait_ge(s["w2"], HC * b + f + 1)
                    for n in range(CC):
                        mm = product(pe, ps[:, n, :], [v[:, f % 2, n * P:(n + 1) * P] for v in hT],
                                     [w[:, f % RING, :] for w in w2], f == 0, f == HC - 1)
                    mm.then_inc(s["d_mm"], 1)

            turns(pe, batch)


def build(nc, a, out):
    scr = {}
    for l in range(2):
        scr[f"kbd{l}"] = nc.dram_tensor(f"kbd{l}_dram", (B, P, GROUPS * HG * KEYS), F32).ap()
        scr[f"vm{l}"] = nc.dram_tensor(f"vm{l}_dram", (B, P, D), F32).ap()
        scr[f"vt{l}"] = nc.dram_tensor(f"vt{l}_dram", (B, TROWS, D), F32).ap()
    scr["delta"] = nc.dram_tensor("delta_dram", (B, P, KEYS), F32).ap()
    scr["x1"] = nc.dram_tensor("x1_dram", (NTOK + CAP, D), F32).ap()
    scr["xw"] = nc.dram_tensor("xw_dram", (NTOK + CAP, XW), F32).ap()
    scr["xs"] = nc.dram_tensor("xs_dram", (NTOK, XS), F32).ap()
    scr["scores"] = nc.dram_tensor("scores_dram", (NTOK,), F32).ap()
    with ExitStack() as ctx:
        c = {}
        constants(nc, ctx, c)
        key_value_phase(nc, a, scr, c)
        with ExitStack() as part:
            def keep(name, shape, dt=F32):
                c[name] = part.enter_context(nc.sbuf_tensor(f"c_{name}", shape, dt))

            keep("expert_rows", [P, E * CC], I32)
            with ExitStack() as gating:
                c["logits"] = gating.enter_context(nc.sbuf_tensor("c_logits", [P, NT * E], F32))
                c["top8"] = gating.enter_context(nc.sbuf_tensor("c_top8", [P, NT * TOPK], F32))
                token_phase(nc, 0, a, scr, c, a["x"], scr["x1"])
                expert_slots_phase(nc, a, scr, c)
            expert_phase(nc, a, scr, c)
        with ExitStack() as part:
            def keep(name, shape, dt=F32):
                c[name] = part.enter_context(nc.sbuf_tensor(f"c_{name}", shape, dt))

            keep("scores", [P, NT])
            token_phase(nc, 1, a, scr, c, scr["x1"], out)
            keep("hw1", [P, DC, HEAVY])
            keep("hw2", [P, HC, D])
            keep("hb1", [P, HC])
            keep("hb2", [P, D])
            keep("hgam", [P, DC])
            keep("na", [P, B])
            keep("heavy_rows", [P, B, CC], I32)
            c["hw_in"] = part.enter_context(nc.semaphore("heavy_weights_in"))
            routing_phase(nc, a, scr, c)
            heavy_phase(nc, a, scr, c, out)


def kernel(**inputs):
    import numpy as np
    import concourse.bacc as bacc
    from concourse.bass_utils import run_bass_kernel_spmd

    def turned(v):
        return np.ascontiguousarray(np.swapaxes(np.asarray(v), -1, -2))

    host = {
        "x": np.asarray(inputs["x"]).reshape(NTOK, D),
        "ctxT": turned(inputs["ctx_1024"]),
        "tau": np.asarray(inputs["condB_tau"]),
        "delta": np.asarray(inputs["fside_BxS2_0"]),
        "gateT": turned(inputs["L0_ffn_gate_weight"]),
        "gate_upT": turned(inputs["L0_ffn_gate_up_proj"]).reshape(E * D, 2 * F),
        "downT": turned(inputs["L0_ffn_down_proj"]).reshape(E * F, D),
        "routing": np.asarray(inputs["L1_ffn_routing_token"]),
    }
    for l in range(2):
        for n in "qkvo":
            host[f"W{n}T{l}"] = turned(inputs[f"L{l}_xcond_W{n}"])
            host[f"b{n}{l}"] = np.asarray(inputs[f"L{l}_xcond_b{n}"])
    for n in ("light", "heavy"):
        for m in ("gamma", "w1", "b1", "w2", "b2"):
            host[f"{n}_{m}"] = np.asarray(inputs[f"L1_ffn_{n}_{m}"])

    nc = bacc.Bacc("TRN2", target_bir_lowering=False, num_devices=1)
    arrays, a = {}, {}
    for name, v in host.items():
        v = np.ascontiguousarray(v)
        arrays[f"in_{name}"] = v
        a[name] = nc.dram_tensor(f"in_{name}", v.shape, mybir.dt.from_np(v.dtype), kind="ExternalInput").ap()
    out = nc.dram_tensor("out_rows", (NTOK, D), F32, kind="ExternalOutput").ap()
    build(nc, a, out)
    r = run_bass_kernel_spmd(nc, [arrays], core_ids=[0])
    return r.results[0]["out_rows"].reshape(B, SEQ, D)
```
